# Optimizing a Trainium2 kernel written in Bass

```python
import numpy as np
import jax
import jax.numpy as jnp

def _softmax(x, axis=-1):
    return jax.nn.softmax(x, axis=axis)

def _gelu(x):
    return jax.nn.gelu(x, approximate=True)

def _silu(x):
    return jax.nn.silu(x)

def _sigmoid(x):
    return jax.nn.sigmoid(x)

def _layernorm(x, axis=-1, eps=1e-05):
    m = jnp.mean(x, axis=axis, keepdims=True)
    v = jnp.var(x, axis=axis, keepdims=True)
    return (x - m) / jnp.sqrt(v + eps)

def _scatter_add(tgt, idx, src, axis=0):
    return tgt.at[idx].add(src)

def _segment_sum(src, seg, n):
    return jax.ops.segment_sum(src, seg, n)
kernel_name = 'mk_seq_postln_d2_jaxref_r8_bbd722'

def setup_inputs(seed: int=0):
    np.random.seed(seed)
    _w = jnp.asarray

    def _L0_attn_setup():
        import jax, jax.numpy as jnp
        import numpy as np
        B, C, L = (64, 64, 512)
        key = jax.random.key(seed)
        x = jax.random.normal(key, (B, C, L), dtype=jnp.float32)
        return {'x': x}
    _L0_attn_in = _L0_attn_setup()

    def _L0_ffn_setup():
        import jax, jax.numpy as jnp
        import numpy as np
        B, S, D = (4, 256, 512)
        NUM_EXPERTS, TOP_K = (3, 2)

        def _expert_outputs(h, w1, b1, w2, b2):
            pre = jnp.einsum('bsd,edf->ebsf', h, w1) + b1[:, None, None, :]
            act = jnp.stack([jnp.tanh(pre[0]), jax.nn.gelu(pre[1], approximate=False), jax.nn.silu(pre[2])])
            return jnp.einsum('ebsf,efd->ebsd', act, w2) + b2[:, None, None, :]
        key = jax.random.key(seed)
        ks = jax.random.split(key, 8)
        scale_in = 1.0 / np.sqrt(D)
        scale_gate = 1.0 / np.sqrt(D + 1)
        return {'h': jax.random.normal(ks[0], (B, S, D), dtype=jnp.float32), 'gate_w': jax.random.uniform(ks[1], (D + 1, NUM_EXPERTS), minval=-scale_gate, maxval=scale_gate, dtype=jnp.float32), 'gate_b': jnp.zeros((NUM_EXPERTS,), dtype=jnp.float32), 'w1': jax.random.uniform(ks[2], (NUM_EXPERTS, D, D), minval=-scale_in, maxval=scale_in, dtype=jnp.float32), 'b1': jnp.zeros((NUM_EXPERTS, D), dtype=jnp.float32), 'w2': jax.random.uniform(ks[3], (NUM_EXPERTS, D, D), minval=-scale_in, maxval=scale_in, dtype=jnp.float32), 'b2': jnp.zeros((NUM_EXPERTS, D), dtype=jnp.float32)}
    _L0_ffn_in = _L0_ffn_setup()

    def _L1_attn_setup():
        import jax, jax.numpy as jnp
        import numpy as np
        HIDDEN = 512
        NUM_HEADS = 32
        HEAD_DIM = HIDDEN // NUM_HEADS

        def _fp8_roundtrip(x):
            return x.astype(jnp.float8_e4m3fn).astype(jnp.float32)
        key = jax.random.key(seed)
        ks = jax.random.split(key, 10)
        B, S = (2, 512)
        hidden_states = jax.random.normal(ks[0], (B, S, HIDDEN), dtype=jnp.float32)
        scale = 0.02

        def lin(kw, kb):
            w = jax.random.normal(kw, (HIDDEN, HIDDEN), dtype=jnp.float32) * scale
            b = jax.random.normal(kb, (HIDDEN,), dtype=jnp.float32) * scale
            return (w, b)
        wq, bq = lin(ks[1], ks[2])
        wk, bk = lin(ks[3], ks[4])
        wv, bv = lin(ks[5], ks[6])
        wl, bl = lin(ks[7], ks[8])
        wq, bq = (_fp8_roundtrip(wq), _fp8_roundtrip(bq))
        wk, bk = (_fp8_roundtrip(wk), _fp8_roundtrip(bk))
        wv, bv = (_fp8_roundtrip(wv), _fp8_roundtrip(bv))
        return {'hidden_states': hidden_states, 'wq': wq, 'bq': bq, 'wk': wk, 'bk': bk, 'wv': wv, 'bv': bv, 'wl': wl, 'bl': bl}
    _L1_attn_in = _L1_attn_setup()

    def _L1_ffn_setup():
        import jax, jax.numpy as jnp
        import numpy as np
        HID, INT, LAT, NE, K = (512, 1024, 256, 8, 2)
        LN_EPS = 1e-05

        def _layernorm(x, gamma, beta):
            mu = jnp.mean(x, axis=-1, keepdims=True)
            var = jnp.var(x, axis=-1, keepdims=True)
            return (x - mu) * jax.lax.rsqrt(var + LN_EPS) * gamma + beta
        key = jax.random.key(seed)
        ks = jax.random.split(key, 8)
        s = lambda d: 1.0 / np.sqrt(d)
        return {'hidden_states': jax.random.normal(ks[0], (4, 256, HID), jnp.float32), 'gate_w': jax.random.normal(ks[1], (HID, NE), jnp.float32) * s(HID), 'up_w': jax.random.normal(ks[2], (HID, INT), jnp.float32) * s(HID), 'down_w': jax.random.normal(ks[3], (INT, HID), jnp.float32) * s(INT), 'fc1_w': jax.random.normal(ks[4], (HID, LAT), jnp.float32) * s(HID), 'fc2_w': jax.random.normal(ks[5], (LAT, HID), jnp.float32) * s(LAT), 'expert_w': jax.random.normal(ks[6], (LAT, LAT), jnp.float32), 'ln_gamma': jnp.ones((HID,), jnp.float32), 'ln_beta': jnp.zeros((HID,), jnp.float32)}
    _L1_ffn_in = _L1_ffn_setup()
    _d = {'L0_attn_x': _L0_attn_in['x'], 'L0_ffn_gate_w': _L0_ffn_in['gate_w'], 'L0_ffn_gate_b': _L0_ffn_in['gate_b'], 'L0_ffn_w1': _L0_ffn_in['w1'], 'L0_ffn_b1': _L0_ffn_in['b1'], 'L0_ffn_w2': _L0_ffn_in['w2'], 'L0_ffn_b2': _L0_ffn_in['b2'], 'L1_attn_wq': _L1_attn_in['wq'], 'L1_attn_bq': _L1_attn_in['bq'], 'L1_attn_wk': _L1_attn_in['wk'], 'L1_attn_bk': _L1_attn_in['bk'], 'L1_attn_wv': _L1_attn_in['wv'], 'L1_attn_bv': _L1_attn_in['bv'], 'L1_attn_wl': _L1_attn_in['wl'], 'L1_attn_bl': _L1_attn_in['bl'], 'L1_ffn_gate_w': _L1_ffn_in['gate_w'], 'L1_ffn_up_w': _L1_ffn_in['up_w'], 'L1_ffn_down_w': _L1_ffn_in['down_w'], 'L1_ffn_fc1_w': _L1_ffn_in['fc1_w'], 'L1_ffn_fc2_w': _L1_ffn_in['fc2_w'], 'L1_ffn_expert_w': _L1_ffn_in['expert_w'], 'L1_ffn_ln_gamma': _L1_ffn_in['ln_gamma'], 'L1_ffn_ln_beta': _L1_ffn_in['ln_beta']}
    _x0 = _d['L0_attn_x']
    _d['L0_attn_x'] = jax.random.normal(jax.random.fold_in(jax.random.key(seed), 1), (4, 512, 512), dtype=_x0.dtype)
    del _x0
    return _d

def reference(L0_attn_x, L0_ffn_gate_w, L0_ffn_gate_b, L0_ffn_w1, L0_ffn_b1, L0_ffn_w2, L0_ffn_b2, L1_attn_wq, L1_attn_bq, L1_attn_wk, L1_attn_bk, L1_attn_wv, L1_attn_bv, L1_attn_wl, L1_attn_bl, L1_ffn_gate_w, L1_ffn_up_w, L1_ffn_down_w, L1_ffn_fc1_w, L1_ffn_fc2_w, L1_ffn_expert_w, L1_ffn_ln_gamma, L1_ffn_ln_beta):

    def _L0_attn_ref(x):
        import jax, jax.numpy as jnp
        import numpy as np
        B, C, L = (64, 64, 512)
        b, c, l = x.shape
        q = jnp.transpose(x, (2, 0, 1))
        scale = jnp.asarray(c, x.dtype) ** 0.5
        scores = jnp.einsum('lnc,lmc->lnm', q, q) / scale
        prob = jax.nn.softmax(scores, axis=-1)
        msg = jnp.einsum('lnm,lmc->lnc', prob, q)
        return x + jnp.transpose(msg, (1, 2, 0))

    def _L0_ffn_ref(h, gate_w, gate_b, w1, b1, w2, b2):
        import jax, jax.numpy as jnp
        import numpy as np
        B, S, D = (4, 256, 512)
        NUM_EXPERTS, TOP_K = (3, 2)

        def _expert_outputs(h, w1, b1, w2, b2):
            pre = jnp.einsum('bsd,edf->ebsf', h, w1) + b1[:, None, None, :]
            act = jnp.stack([jnp.tanh(pre[0]), jax.nn.gelu(pre[1], approximate=False), jax.nn.silu(pre[2])])
            return jnp.einsum('ebsf,efd->ebsd', act, w2) + b2[:, None, None, :]
        b, s, d = h.shape
        vision_len = int(s * 0.3)
        text_strength = jnp.mean(jnp.abs(h[:, vision_len:, :]), axis=(1, 2), keepdims=True)
        vision_strength = jnp.mean(jnp.abs(h[:, :vision_len, :]), axis=(1, 2), keepdims=True)
        modality_ratio = text_strength / (vision_strength + 1e-08)
        modality_ratio = jnp.broadcast_to(modality_ratio, (b, s, 1))
        router_input = jnp.concatenate([h, modality_ratio], axis=-1)
        gate_logits = router_input @ gate_w + gate_b
        gate_scores = jax.nn.softmax(gate_logits, axis=-1)
        top_val, top_idx = jax.lax.top_k(gate_scores, TOP_K)
        top_val = top_val / (jnp.sum(top_val, axis=-1, keepdims=True) + 1e-08)
        expert_out = _expert_outputs(h, w1, b1, w2, b2)
        moe_out = jnp.zeros_like(h)
        batch_idx = jnp.arange(b)
        for i in range(TOP_K):
            j = top_idx[:, 0, i]
            out_i = expert_out[j, batch_idx]
            moe_out = moe_out + top_val[..., i:i + 1] * out_i
        return moe_out

    def _L1_attn_ref(hidden_states, wq, bq, wk, bk, wv, bv, wl, bl):
        import jax, jax.numpy as jnp
        import numpy as np
        HIDDEN = 512
        NUM_HEADS = 32
        HEAD_DIM = HIDDEN // NUM_HEADS

        def _fp8_roundtrip(x):
            return x.astype(jnp.float8_e4m3fn).astype(jnp.float32)
        B, S, E = hidden_states.shape
        H, D = (NUM_HEADS, HEAD_DIM)
        q = (hidden_states @ wq.T + bq).reshape(B, S, H, D)
        k = (hidden_states @ wk.T + bk).reshape(B, S, H, D)
        v = (hidden_states @ wv.T + bv).reshape(B, S, H, D)
        latent = hidden_states @ wl.T + bl
        scores = jnp.einsum('bshd,bstd->bsht', q, k) / np.sqrt(D).astype(np.float32)
        probs = jax.nn.softmax(scores, axis=-1)
        context = jnp.einsum('bsht,bstd->bshd', probs, v).reshape(B, S, E)
        return context

    def _L1_ffn_ref(hidden_states, gate_w, up_w, down_w, fc1_w, fc2_w, expert_w, ln_gamma, ln_beta):
        import jax, jax.numpy as jnp
        import numpy as np
        HID, INT, LAT, NE, K = (512, 1024, 256, 8, 2)
        LN_EPS = 1e-05

        def _layernorm(x, gamma, beta):
            mu = jnp.mean(x, axis=-1, keepdims=True)
            var = jnp.var(x, axis=-1, keepdims=True)
            return (x - mu) * jax.lax.rsqrt(var + LN_EPS) * gamma + beta
        logits = jnp.einsum('bsh,he->bse', hidden_states, gate_w)
        routing_weights, selected_experts = jax.lax.top_k(logits, K)
        h = jax.nn.relu(jnp.einsum('bsh,hi->bsi', hidden_states, up_w)) ** 2
        shared_out = jnp.einsum('bsi,ih->bsh', h, down_w)
        x_latent = jnp.einsum('bsh,hl->bsl', hidden_states, fc1_w)
        expert_out = jnp.einsum('bsl,lm->bsm', x_latent, expert_w)
        moe_out = expert_out * jnp.sum(routing_weights, axis=-1, keepdims=True)
        routed_out = jnp.einsum('bsl,lh->bsh', moe_out, fc2_w)
        return _layernorm(shared_out + routed_out, ln_gamma, ln_beta)
    x = L0_attn_x
    x = _layernorm(x + _L0_attn_ref(x), axis=-1)
    x = _layernorm(x + _L0_ffn_ref(x, L0_ffn_gate_w, L0_ffn_gate_b, L0_ffn_w1, L0_ffn_b1, L0_ffn_w2, L0_ffn_b2), axis=-1)
    x = _layernorm(x + _L1_attn_ref(x, L1_attn_wq, L1_attn_bq, L1_attn_wk, L1_attn_bk, L1_attn_wv, L1_attn_bv, L1_attn_wl, L1_attn_bl), axis=-1)
    x = _layernorm(x + _L1_ffn_ref(x, L1_ffn_gate_w, L1_ffn_up_w, L1_ffn_down_w, L1_ffn_fc1_w, L1_ffn_fc2_w, L1_ffn_expert_w, L1_ffn_ln_gamma, L1_ffn_ln_beta), axis=-1)
    return x

_drawn_inputs = setup_inputs


def setup_inputs(seed=0):
    import zlib

    import numpy as np

    out = dict(_drawn_inputs(seed))
    spreads = {'L0_ffn_gate_b': (0.0, 0.1),
     'L0_ffn_b1': (0.0, 0.1),
     'L0_ffn_b2': (0.0, 0.1),
     'L1_ffn_ln_gamma': (1.0, 0.2),
     'L1_ffn_ln_beta': (0.0, 0.1)}
    factors = {'L1_attn_wq': 2.808,
     'L1_attn_bq': 8.0,
     'L1_attn_wk': 2.676,
     'L1_attn_bk': 8.0,
     'L1_attn_bv': 8.0}
    for name, (base, spread) in spreads.items():
        noise = np.random.default_rng([zlib.crc32(name.encode()), seed]).standard_normal(out[name].shape)
        drawn = base * np.exp(spread * noise) if base else spread * noise
        out[name] = jnp.asarray(drawn.astype(out[name].dtype))
    for name, factor in factors.items():
        out[name] = (out[name] * factor).astype(out[name].dtype)
    return out
```

```python
from contextlib import ExitStack

import concourse.bass as bass
from concourse import mybir

F32 = mybir.dt.float32
F32R = mybir.dt.float32r
I32 = mybir.dt.int32
ALU = mybir.AluOpType
ACT = mybir.ActivationFunctionType
X = mybir.AxisListType.X

P = 128
B = 4
S = 512
D = 512
KB = D // P
TB = S // P
NT = B * TB
E = 3
H, DH = 32, 16
INT, LAT, NE = 1024, 256, 8
NU, NL = INT // P, LAT // P
VIS = int(S * 0.3)
EPS = 1e-5
RSQRT_MAGIC = 0x5F3759DF


class Chain:

    def __init__(self, eng, sem):
        self.eng, self.sem, self.base, self.i, self.per, self.k = eng, sem, 0, 0, 0, 0

    def link(self, ins):
        self.k += 1
        ins.then_inc(self.sem, 1)
        self.eng.wait_ge(self.sem, self.i * self.per + (self.base + self.k))

    def begin(self, i=0, per=0):
        self.i, self.per, self.k = i, per, 0

    def end(self, times=1):
        assert self.per in (0, self.k), f"links in the loop's body: {self.k}"
        self.base += times * self.k
        self.i = self.per = self.k = 0


def build_program(nc, x, gate_w, gate_b, w1, b1, w2, b2, wq, bq, wk, bk, wv, bv,
                  gate8_w, up_w, down_w, fc1_w, fc2_w, expert_w, gamma, beta, out):
    with ExitStack() as ctx:
        base = (nc.sbuf_base + 31) // 32 * 32
        top = nc.sbuf_usable_end

        def at(name, shape, offset, dt=F32):
            size = 4
            for n in shape[1:]:
                size *= n
            assert base + offset + size <= top, name
            return nc.alloc_sbuf_tensor_at(name, shape, dt, offset=base + offset)

        def sem(name):
            return ctx.enter_context(nc.semaphore(name))

        K = 1024
        RES = 0
        XT_AT = 32 * K
        ACT_AT = 48 * K
        W_AT = 80 * K
        MISC = 176 * K
        xs = at("xs", [P, NT, D], RES)
        xT = at("xT", [P, KB, B, S], XT_AT)
        yT = at("yT", [P, 2, B, S], XT_AT + 32 * K)
        raw = at("raw", [P, 2, KB, D], MISC)
        dump = at("dump", [P, S], MISC + 16 * K)
        dump2 = at("dump2", [P, S], MISC + 18 * K)
        wf = at("wf", [P, 2, E, 2, KB, D], W_AT, F32R)
        stage = at("stage", [P, TB, D], MISC)
        acc = at("acc", [P, TB, D], MISC + 8 * K)
        act32 = at("act32", [P, 2, S], MISC + 16 * K)
        gwp = at("gwp", [P, 2, KB, P], MISC + 20 * K, F32R)
        rowsE = at("rowsE", [E, S], MISC + 24 * K)
        b2s = at("b2s", [E, D], MISC + 26 * K)
        small2 = at("small2", [P, 256], MISC + 28 * K)
        xth = at("xth", [P, 2, KB, S], XT_AT, F32R)
        a2 = at("a2", [P, 2, 2, KB, S], ACT_AT, F32R)
        rawq = at("rawq", [P, 3, KB, D], W_AT)
        wqkv = at("wqkv", [P, 3, 2, KB, D], W_AT + 32 * K, F32R)
        vT = at("vT", [P, 2, DH + 1, 32], W_AT + 24 * K)
        xt3 = at("xt3", [P, 2, KB, 2 * P], XT_AT, F32R)
        vs = at("vs", [P, 2, D], XT_AT + 8 * K)
        qT = at("qT", [P, 2, H, 32], ACT_AT)
        kT = at("kT", [P, 2, H, 32], ACT_AT + 8 * K)
        sh = at("sh", [P, 2, 32, H], ACT_AT + 16 * K)
        ctxs = sh[:, :, :, 0:DH]
        pT = at("pT", [P, 2, 32, H], ACT_AT + 24 * K)
        stage3 = at("stage3", [P, 2, D], MISC)
        bq_b = at("bq_b", [P, D], MISC + 4 * K)
        bk_b = at("bk_b", [P, D], MISC + 6 * K)
        acc3 = at("acc3", [P, 2, D], MISC + 8 * K)
        attn = at("attn", [P, 2, D], MISC + 12 * K)
        bv_b = at("bv_b", [P, D], MISC + 16 * K)
        qs = at("qs", [P, 2, D + DH], MISC + 18 * K)
        ks = at("ks", [P, 2, D + DH], MISC + 18 * K + 4224)
        rawu = at("rawu", [P, KB, INT], W_AT)
        raw1 = at("raw1", [P, KB, LAT], W_AT + 16 * K)
        raw2 = at("raw2", [P, NL, D], W_AT + 20 * K)
        rawe = at("rawe", [P, NL, LAT], W_AT + 29 * K)
        rawd = at("rawd", [P, NU, D], W_AT + 64 * K)
        wup = at("wup", [P, 2, KB, INT], W_AT + 32 * K, F32R)
        wdn = at("wdn", [P, 2, NU, D], W_AT, F32R)
        wf1 = at("wf1", [P, 2, KB, LAT], W_AT + 80 * K, F32R)
        wef = at("wef", [P, 2, NL, D], W_AT + 88 * K, F32R)
        lat = at("lat", [P, 2, NL, S], W_AT + 64 * K, F32R)
        gam_b = at("gam_b", [P, D], W_AT + 72 * K)
        bet_b = at("bet_b", [P, D], W_AT + 74 * K)
        rows8 = at("rows8", [NE, S], W_AT + 76 * K)
        expT = at("expT", [P, NL, LAT], XT_AT)
        hh = at("hh", [P, NU, 2, S], ACT_AT, F32R)
        stage4 = at("stage4", [P, TB, D], MISC)
        acc4 = at("acc4", [P, TB, D], MISC + 8 * K)
        relu = (at("relu0", [P, S], MISC + 16 * K), at("relu1", [P, S], MISC + 26 * K))
        g8p = at("g8p", [P, 2, KB, P], MISC + 18 * K, F32R)
        sq32 = at("sq32", [P, S], MISC + 22 * K)
        SM = MISC + 30 * K
        ident = at("ident", [P, P], SM)
        ones = at("ones", [P, P], SM + 512)
        small = at("small", [P, 180], SM + 1024)

        ps = ctx.enter_context(nc.psum_tensor("ps", [P, 8, 512], F32))

        s_x = [sem(f"x_row{n}_loaded") for n in range(B)]
        s_raw = [sem(f"raw{n}_loaded") for n in range(2)]
        s_ident = sem("ident_written")
        s_xt_ps = sem("x_transposed_in_psum")
        s_xt_a = sem("xT_copied_by_scalar")
        s_xt_v = sem("xT_copied_by_vector")
        s_sq = sem("squares_summed")
        s_prod = sem("score_products_ready")
        s_pexp_in = sem("shifted_scores_ready")
        s_pexp = sem("score_exps_ready")
        s_mixw = sem("mix_weights_ready")
        s_y0 = sem("first_mix_term_ready")
        s_y = sem("mixed_rows_ready")
        s_yt = sem("mixed_rows_transposed_in_psum")
        s_ycp = sem("mixed_rows_copied_back")
        s_ln1 = sem("ln1_scale_ready")
        s_x1 = sem("x1_tiles_written")
        s_whi = sem("w_high_written")
        s_wlo = sem("w_low_written")
        s_vch = sem("vector_chain")
        s_ach = sem("scalar_chain")
        s_gch = sem("pool_chain")
        s_out = sem("out_stored")
        s_settled = sem("settled")
        m_consts = sem("m_consts_loaded")
        m_gwp = sem("m_gate_weights_split")
        m_stage = sem("m_x_staged")
        m_T = sem("m_xT_in_psum")
        m_Thi = sem("m_xT_high_written")
        m_Tlo = sem("m_xT_low_written")
        m_abs = sem("m_abs_sums_ready")
        m_stat = sem("m_stat_terms_ready")
        m_statps = sem("m_stat_sums_in_psum")
        m_gbias = sem("m_gate_bias_ready")
        m_gps = sem("m_gate_rows_in_psum")
        m_rows = sem("m_logit_rows_copied")
        m_lps = sem("m_logits_in_psum")
        m_shift = sem("m_logits_shifted")
        m_exp = sem("m_exps_ready")
        m_prob = sem("m_probs_ready")
        m_t0 = sem("m_first_token_in_psum")
        m_coef = sem("m_coefs_ready")
        m_cTps = sem("m_coef_rows_in_psum")
        m_cT = sem("m_coef_rows_copied")
        m_bc = sem("m_bias_mix_in_psum")
        m_acc0 = sem("m_residual_added")
        m_F = sem("m_hidden_in_psum")
        m_A = sem("m_act_written")
        m_hi = sem("m_act_high_written")
        m_lo = sem("m_act_buffers_done_by_pool")
        m_O = sem("m_expert_out_in_psum")
        m_Oacc = sem("m_out_banks_free")
        m_x2 = sem("m_x2_tiles_written")
        a_raw = [sem(f"a_raw_{n}_loaded") for n in "qkv"]
        a_bias = sem("a_biases_loaded")
        a_wps = sem("a_weights_transposed_in_psum")
        a_whi = sem("a_w_high_written")
        a_wlo = sem("a_w_low_written")
        a_const = sem("a_padding_and_ones_written")
        a_stage = sem("a_x_staged")
        a_T = sem("a_xT_in_psum")
        a_Thi = sem("a_xT_high_written")
        a_Tlo = sem("a_xT_low_written")
        a_proj = sem("a_projection_in_psum")
        a_evac = sem("a_projection_copied")
        a_qk = sem("a_qT_kT_written")
        a_vT = sem("a_vT_written")
        a_S = sem("a_scores_in_psum")
        a_shift = sem("a_scores_shifted")
        a_exp = sem("a_exps_ready")
        a_PT = sem("a_probs_transposed")
        a_PV = sem("a_context_in_psum")
        a_ctx = sem("a_context_normalised")
        a_x3 = sem("a_x3_tiles_written")
        p_rawu = sem("p_up_loaded")
        p_raws = sem("p_small_weights_loaded")
        p_rawd = sem("p_down_loaded")
        p_gb = sem("p_gamma_beta_loaded")
        p_whi = sem("p_w_high_written")
        p_wlo = sem("p_w_low_written")
        p_eTps = sem("p_expT_in_psum")
        p_eT = sem("p_expT_copied")
        p_ef = sem("p_expert_fc2_in_psum")
        p_efhi = sem("p_expert_fc2_high")
        p_eflo = sem("p_expert_fc2_low")
        p_g8 = sem("p_gate_split")
        p_stage = sem("p_x_staged")
        p_T = sem("p_xT_in_psum")
        p_Thi = sem("p_xT_high_written")
        p_Tlo = sem("p_xT_low_written")
        p_gps = sem("p_gate_rows_in_psum")
        p_rows = sem("p_gate_rows_copied")
        p_lps = sem("p_logits_in_psum")
        p_top = sem("p_logits_copied")
        p_U = sem("p_up_in_psum")
        p_relu = sem("p_relu_written")
        p_hi = sem("p_square_high_written")
        p_lo = sem("p_square_low_written")
        p_L = sem("p_latent_in_psum")
        p_Lhi = sem("p_latent_high_written")
        p_Llo = sem("p_latent_low_written")
        p_R = sem("p_routed_in_psum")
        p_Radd = sem("p_routed_added")
        p_D = sem("p_down_in_psum")
        p_Dadd = sem("p_down_banks_free")
        p_xb = sem("p_beta_added_to_residual")
        p_y = sem("p_output_tiles_ready")

        def bc(ap, shape):
            return ap.to_broadcast(shape) if not isinstance(ap, bass.AP) else ap.broadcast_to(shape)

        sc = small[:, 0:64].rearrange("p (l n m) -> p l n m", l=KB, n=B)
        mx = small[:, 64:80]
        stats = small[:, 80:86]
        mv = small[:, 86:118].rearrange("p (t c) -> p t c", c=2)
        rs = small[:, 118:134]
        nm = small[:, 134:150]
        hv = small[:, 150:166]
        magic = small[:, 166:168].bitcast(I32)

        absum = small2[:, 0:TB]
        statin = small2[:, 4:12].rearrange("p (t c) -> p t c", c=2)
        vmask = small2[:, 12:20].rearrange("p (t c) -> p t c", c=2)
        gbias = small2[:, 20:21]
        gw_last = small2[:, 21:22]
        gb_col = small2[:, 22:23]
        ratio = small2[:, 23:26]
        gwraw = small2[:, 26:38].rearrange("p (k e) -> p k e", e=E)
        b1c = small2[:, 38:50].rearrange("p (e f) -> p e f", f=KB)
        pr = small2[:, 50:62].rearrange("p (t e) -> p t e", e=E)
        coef = small2[:, 62:74].rearrange("p (t e) -> p t e", e=E)
        tmp = small2[:, 74:86].rearrange("p (t e) -> p t e", e=E)
        top = small2[:, 86:94].rearrange("p (i t) -> p i t", i=2)
        sel = small2[:, 94:100].rearrange("p (i e) -> p i e", i=2)
        cmp3 = small2[:, 100:103]
        rank = small2[:, 103:106]
        tA, tB = small2[:, 106:110], small2[:, 110:114]
        stats4 = small2[:, 114:138].rearrange("p (t c) -> p t c", c=6)
        OB = 3
        mx3 = small2[:, 140:204].rearrange("p (u i) -> p u i", u=2)
        NP2 = NT // 2
        PROJ_BANK = (6, 7, 4, 5, 6, 7)
        G = P // 32
        g8raw = small2[:, 204:236].rearrange("p (k e) -> p k e", e=NE)
        logit8 = mx3.rearrange("p u i -> p (u i)")[:, 0:TB * NE].rearrange("p (t e) -> p t e", e=NE)
        top8 = mx3.rearrange("p u i -> p (u i)")[:, TB * NE:2 * TB * NE].rearrange("p (t e) -> p t e", e=NE)
        route = tA
        FUNCS = (ACT.Tanh, ACT.Gelu, ACT.Silu)

        block = ctx.enter_context(nc.Block())

        WB = [(j, e) for e in range(E) for j in range(2)]

        @block.sync
        def _(sp):
            for n in range(B):
                sp.dma_start(xs[:, TB * n:TB * n + TB, :],
                             x[n].rearrange("(t p) d -> p t d", p=P)).then_inc(s_x[n], 16)
            for q, (j, e) in enumerate(WB):
                if q >= 2:
                    sp.wait_ge(s_whi, q - 1)
                    sp.wait_ge(s_wlo, q - 1)
                sp.dma_start(raw[:, q % 2], (w1, w2)[j][e].rearrange("(k p) n -> p k n", p=P)
                             ).then_inc(s_raw[q % 2], 16)
            with nc.allow_non_contiguous_dma("small columns"):
                sp.dma_start(gwraw, gate_w[0:D].rearrange("(k p) e -> p k e", p=P)).then_inc(m_consts, 16)
                sp.dma_start(gw_last[0:E], gate_w[D:D + 1].rearrange("o e -> e o")).then_inc(m_consts, 16)
                sp.dma_start(gb_col[0:E], gate_b.rearrange("(e o) -> e o", o=1)).then_inc(m_consts, 16)
                sp.dma_start(b1c, b1.rearrange("e (f p) -> p e f", p=P)).then_inc(m_consts, 16)
                sp.dma_start(b2s[:], b2).then_inc(m_consts, 16)
            sp.wait_ge(s_whi, 2 * E)
            sp.wait_ge(s_wlo, 2 * E)
            sp.wait_ge(s_x1, NT)
            sp.dma_start(stage[:], xs[:, 0:TB]).then_inc(m_stage, 16)
            with sp.Fori(0, B - 1) as c:
                sp.wait_ge(m_abs, c + 1)
                sp.sem_inc(s_settled, 1)
                sp.dma_start(stage[:], xs[:, bass.ds(TB * c + TB, TB)]).then_inc(m_stage, 16)
            C3 = B - 1
            sp.wait_ge(m_F, E * KB * C3 + KB)
            sp.dma_start(rawq[:, 0], wq.rearrange("(o p) i -> p o i", p=P)).then_inc(a_raw[0], 16)
            sp.dma_start(rawq[:, 1], wk.rearrange("(o p) i -> p o i", p=P)).then_inc(a_raw[1], 16)
            sp.wait_ge(m_F, E * KB * C3 + 2 * KB)
            sp.dma_start(rawq[:, 2], wv.rearrange("(o p) i -> p o i", p=P)).then_inc(a_raw[2], 16)
            sp.wait_ge(m_lo, E * KB * B + 2)
            sp.wait_ge(m_abs, B)
            sp.dma_start(bq_b[:], bq.partition_broadcast(P)).then_inc(a_bias, 16)
            sp.dma_start(bk_b[:], bk.partition_broadcast(P)).then_inc(a_bias, 16)
            sp.dma_start(bv_b[:], bv.partition_broadcast(P)).then_inc(a_bias, 16)
            sp.dma_start(stage3[:], xs[:, 0:2]).then_inc(a_stage, 16)
            sp.wait_ge(a_wps, 3 * KB)
            sp.dma_start(rawu[:], up_w.rearrange("(k p) n -> p k n", p=P)).then_inc(p_rawu, 16)
            sp.dma_start(raw1[:], fc1_w.rearrange("(k p) n -> p k n", p=P)).then_inc(p_raws, 16)
            sp.dma_start(raw2[:], fc2_w.rearrange("(k p) n -> p k n", p=P)).then_inc(p_raws, 16)
            sp.dma_start(rawe[:], expert_w.rearrange("(k p) n -> p k n", p=P)).then_inc(p_raws, 16)
            sp.dma_start(g8raw, gate8_w.rearrange("(k p) n -> p k n", p=P)).then_inc(p_raws, 16)
            sp.wait_ge(m_x2, NT)
            with sp.Fori(0, NP2 - 1) as p:
                sp.wait_ge(a_T, 2 * p + 2)
                sp.sem_inc(s_settled, 1)
                sp.dma_start(stage3[:], xs[:, bass.ds(2 * p + 2, 2)]).then_inc(a_stage, 16)
            sp.wait_ge(a_proj, 6 * NP2)
            sp.dma_start(rawd[:], down_w.rearrange("(k p) n -> p k n", p=P)).then_inc(p_rawd, 16)
            sp.wait_ge(a_T, 2 * NP2)
            sp.wait_ge(a_evac, 6 * NP2)
            sp.wait_ge(a_x3, TB)
            sp.dma_start(stage4[:], xs[:, 0:TB]).then_inc(p_stage, 16)
            sp.wait_ge(p_wlo, KB + 1 + TB)
            sp.dma_start(gam_b[:], gamma.partition_broadcast(P)).then_inc(p_gb, 16)
            sp.dma_start(bet_b[:], beta.partition_broadcast(P)).then_inc(p_gb, 16)
            sp.wait_ge(a_x3, NT)
            out_tiles = out.rearrange("b (t p) d -> (b t) p d", p=P)

            def store(c):
                for t in range(TB):
                    sp.wait_ge(p_y, TB * c + (t + 1))
                    sp.sem_inc(s_settled, 1)
                    sp.dma_start(out_tiles[TB * c + t], acc4[:, t]).then_inc(s_out, 16)

            with sp.Fori(0, B - 1) as c:
                sp.wait_ge(p_T, KB * c + KB)
                sp.sem_inc(s_settled, 1)
                sp.dma_start(stage4[:], xs[:, bass.ds(TB * c + TB, TB)]).then_inc(p_stage, 16)
                store(c)
            store(B - 1)
            sp.wait_ge(s_out, 16 * NT)

        @block.gpsimd
        def _(pool):
            ch = Chain(pool, s_gch)
            ch.link(pool.memset(ident[:], 0.0))
            pool.affine_select(out=ident[:], in_=ident[:], compare_op=ALU.not_equal, fill=1.0,
                               base=0, pattern=[[-1, P]], channel_multiplier=1).then_inc(s_ident, 1)
            for q, (j, e) in enumerate(WB):
                pool.wait_ge(s_raw[q % 2], 16 * (q // 2 + 1))
                pool.wait_ge(s_whi, q + 1)
                pool.tensor_tensor(wf[:, j, e, 1], raw[:, q % 2], wf[:, j, e, 0].bitcast(F32),
                                   ALU.subtract).then_inc(s_wlo, 1)
            ch.link(pool.memset(ones[:], 1.0))
            ch.link(pool.memset(gwp[:].bitcast(F32), 0.0))
            ch.link(pool.memset(vmask, 0.0))
            for t in range(TB):
                lo = VIS - t * P
                if lo >= P:
                    ch.link(pool.memset(vmask[:, t, 1:2], 1.0 / (VIS * D)))
                elif lo <= 0:
                    ch.link(pool.memset(vmask[:, t, 0:1], 1.0 / ((S - VIS) * D)))
                else:
                    ch.link(pool.memset(vmask[:, t, 1:2], 1.0 / (VIS * D)))
                    ch.link(pool.memset(vmask[:, t, 0:1], 1.0 / ((S - VIS) * D)))
                    ch.link(pool.affine_select(out=vmask[:, t, 1:2], in_=vmask[:, t, 1:2], compare_op=ALU.is_ge,
                                               fill=0.0, base=lo - 1, pattern=[[0, 1]], channel_multiplier=-1))
                    ch.link(pool.affine_select(out=vmask[:, t, 0:1], in_=vmask[:, t, 0:1], compare_op=ALU.is_ge,
                                               fill=0.0, base=-lo, pattern=[[0, 1]], channel_multiplier=1))
            pool.wait_ge(m_consts, 80)
            ch.link(pool.tensor_copy(gwp[:, 0, :, 0:E], gwraw))
            pool.tensor_tensor(gwp[:, 1, :, 0:E], gwraw, gwp[:, 0, :, 0:E].bitcast(F32),
                               ALU.subtract).then_inc(m_gwp, 1)

            def low_halves(c):
                for j in range(E * KB):
                    e, f = j // KB, j % KB
                    pool.wait_ge(m_hi, E * KB * c + (j + 1))
                    pool.tensor_tensor(a2[:, e % 2, 1, f], act32[:, j % 2], a2[:, e % 2, 0, f].bitcast(F32),
                                       ALU.subtract).then_inc(m_lo, 1)

            ch.link(pool.memset(stats4[:, 0, 0:1], 0.0))
            pool.memset(stats4[:, 0, 0:1], 0.0).then_inc(m_lo, 2)
            with pool.Fori(0, B) as c:
                low_halves(c)

            pool.wait_ge(m_gps, B)
            pool.wait_ge(m_bc, TB * B)
            pool.wait_ge(m_F, E * KB * B)
            pool.memset(qs[:, :, D:], 0.0).then_inc(a_const, 1)
            pool.memset(ks[:, :, D:], 0.0).then_inc(a_const, 1)
            pool.memset(vT[:, :, DH, :], 1.0).then_inc(a_const, 1)

            pool.wait_ge(p_raws, 64)
            pool.wait_ge(p_whi, 1)
            pool.tensor_tensor(wf1[:, 1], raw1[:], wf1[:, 0].bitcast(F32), ALU.subtract).then_inc(p_wlo, 1)
            pool.wait_ge(a_qk, 4 * NP2)
            ch.link(pool.memset(g8p[:].bitcast(F32), 0.0))
            ch.link(pool.tensor_copy(g8p[:, 0, :, 0:NE], g8raw))
            pool.tensor_tensor(g8p[:, 1, :, 0:NE], g8raw, g8p[:, 0, :, 0:NE].bitcast(F32),
                               ALU.subtract).then_inc(p_g8, 1)
            for k in range(KB):
                pool.wait_ge(p_whi, k + 2)
                pool.tensor_tensor(wup[:, 1, k], rawu[:, k], wup[:, 0, k].bitcast(F32), ALU.subtract).then_inc(p_wlo, 1)
            pool.wait_ge(a_PV, NP2)
            for k in range(0, NU, 2):
                pool.wait_ge(p_whi, KB + 2 + k // 2)
                pool.tensor_tensor(wdn[:, 1, k:k + 2], rawd[:, k:k + 2], wdn[:, 0, k:k + 2].bitcast(F32),
                                   ALU.subtract).then_inc(p_wlo, 1)

            pool.wait_ge(p_gb, 32)
            with pool.Fori(0, B) as c:
                pool.wait_ge(p_stage, 16 * c + 16)
                for t in range(TB):
                    pool.tensor_tensor(xs[:, TB * c + t], xs[:, TB * c + t], bet_b[:], ALU.add).then_inc(p_xb, 1)

        @block.tensor
        def _(pe):
            pe.wait_ge(s_ident, 1)
            for n in range(B):
                pe.wait_ge(s_x[n], 16)
                for lb in range(KB):
                    job = KB * n + lb
                    if job >= 8:
                        pe.wait_ge(*((s_xt_a, (job - 8) // 2 + 1) if job % 2 == 0 else (s_xt_v, (job - 8) // 2 + 1)))
                    for t in range(TB):
                        mm = pe.transpose(ps[:, job % 8, t * P:(t + 1) * P],
                                          xs[:, TB * n + t, lb * P:(lb + 1) * P], ident[:])
                    mm.then_inc(s_xt_ps, 1)
            for lb in range(KB):
                for n in range(B):
                    job = KB * B + lb * B + n
                    pe.wait_ge(s_y, B * lb + n + 1)
                    if lb >= 2:
                        pe.wait_ge(s_ycp, B * (lb - 2) + n + 1)
                    for t in range(TB):
                        mm = pe.transpose(ps[:, (lb * B + n) % 8, t * P:(t + 1) * P],
                                          yT[:, lb % 2, n, t * P:(t + 1) * P], ident[:])
                    mm.then_inc(s_yt, 1)

            def split3(dst, w_hi, w_lo, x_hi, x_lo, first, last):
                pe.matmul(dst, w_hi, x_hi, start=first, stop=False)
                pe.matmul(dst, w_hi, x_lo, start=False, stop=False)
                return pe.matmul(dst, w_lo, x_hi, start=False, stop=last)

            def m_transposes(c):
                pe.wait_ge(m_stage, 16 * c + 16)
                for k in range(KB):
                    if c is not first_c:
                        pe.wait_ge(m_hi, E * KB * c - (KB - k - 1))
                    for t in range(TB):
                        mm = pe.transpose(ps[:, k, t * P:(t + 1) * P], stage[:, t, k * P:(k + 1) * P], ident[:])
                    mm.then_inc(m_T, 1)

            def m_stats(c):
                pe.wait_ge(m_stat, c + 1)
                for t in range(TB):
                    mm = pe.matmul(ps[:, 7, 0:2], ones[:], statin[:, t], start=(t == 0), stop=(t == TB - 1))
                mm.then_inc(m_statps, 1)

            def m_gate(c):
                pe.wait_ge(m_Thi, KB * c + KB)
                pe.wait_ge(m_Tlo, KB * c + KB)
                pe.wait_ge(m_gbias, c + 1)
                for k in range(KB):
                    mm = split3(ps[:, 7, :], gwp[:, 0, k], gwp[:, 1, k], xth[:, 0, k], xth[:, 1, k],
                                k == 0, k == KB - 1)
                mm.then_inc(m_gps, 1)

            def m_hidden(c, e, f):
                if e == 0 and f == 0:
                    pe.wait_ge(m_Thi, KB * c + KB)
                    pe.wait_ge(m_Tlo, KB * c + KB)
                if e > 0:
                    pe.wait_ge(m_hi, E * KB * c + (KB * (e - 1) + f + 1))
                for k in range(KB):
                    mm = split3(ps[:, f], wf[:, 0, e, 0, k, f * P:(f + 1) * P], wf[:, 0, e, 1, k, f * P:(f + 1) * P],
                                xth[:, 0, k], xth[:, 1, k], k == 0, k == KB - 1)
                mm.then_inc(m_F, 1)

            def m_bias(c, t):
                if t == 0:
                    pe.wait_ge(m_cT, c + 1)
                else:
                    pe.wait_ge(m_acc0, TB * c + t)
                pe.matmul(ps[:, 7, :], rowsE[:, t * P:(t + 1) * P], b2s[:], start=True, stop=True).then_inc(m_bc, 1)

            def m_outp(c, e, t):
                j = e * TB + t
                if t == 0:
                    pe.wait_ge(m_hi, E * KB * c + KB * (e + 1))
                    pe.wait_ge(m_lo, E * KB * c + (KB * (e + 1) + 2))
                pe.wait_ge(m_Oacc, E * TB * c + (j + 1))
                b = 4 + j % OB
                for k in range(KB):
                    mm = split3(ps[:, b], a2[:, e % 2, 0, k, t * P:(t + 1) * P], a2[:, e % 2, 1, k, t * P:(t + 1) * P],
                                wf[:, 1, e, 0, k], wf[:, 1, e, 1, k], k == 0, k == KB - 1)
                mm.then_inc(m_O, 1)

            def m_chunk(c, more):
                for f in range(KB):
                    m_hidden(c, 0, f)
                pe.wait_ge(m_rows, c + 1)
                pe.wait_ge(s_ident, 1)
                for t in range(TB):
                    mm = pe.matmul(ps[:, 7, 4 * t:4 * t + E], rowsE[:, t * P:(t + 1) * P], ident[0:E, 0:E],
                                   start=True, stop=True)
                mm.then_inc(m_lps, 1)
                m_hidden(c, 1, 0)
                m_hidden(c, 1, 1)
                pe.wait_ge(m_prob, c + 1)
                pe.matmul(ps[:, 7, 0:E], ones[0:1, :], pr[0:1, 0, :], start=True, stop=True).then_inc(m_t0, 1)
                m_hidden(c, 1, 2)
                m_hidden(c, 1, 3)
                pe.wait_ge(m_coef, c + 1)
                for t in range(TB):
                    mm = pe.matmul(ps[0:E, 7, t * P:(t + 1) * P], coef[:, t], ident[:], start=True, stop=True)
                mm.then_inc(m_cTps, 1)
                for t in range(TB):
                    m_bias(c, t)
                    m_outp(c, 0, t)
                for f in range(KB):
                    m_hidden(c, 2, f)
                if more:
                    m_transposes(c + 1)
                else:
                    a_weights(0)
                m_outp(c, 1, 0)
                m_outp(c, 1, 1)
                if more:
                    m_stats(c + 1)
                else:
                    a_weights(1)
                m_outp(c, 1, 2)
                m_outp(c, 1, 3)
                if more:
                    m_gate(c + 1)
                else:
                    a_weights(2)
                for t in range(TB):
                    m_outp(c, 2, t)

            def a_weights(j):
                pe.wait_ge(a_raw[j], 16)
                for k in range(KB):
                    if j == 0:
                        pe.wait_ge(m_hi, E * KB * B - (KB - 1 - k))
                    else:
                        pe.wait_ge(a_wlo, KB * (j - 1) + k + 1)
                    for o in range(KB):
                        mm = pe.transpose(ps[:, k, o * P:(o + 1) * P], rawq[:, j, o, k * P:(k + 1) * P], ident[:])
                    mm.then_inc(a_wps, 1)

            first_c = 0
            m_transposes(0)
            pe.wait_ge(m_gwp, 1)
            m_stats(0)
            m_gate(0)
            with pe.Fori(0, B - 1) as c:
                first_c = None
                m_chunk(c, True)
            m_chunk(B - 1, False)

            def a_transposes(p, first=False):
                pe.wait_ge(a_stage, 16 * p + 16)
                if first:
                    pe.wait_ge(m_Oacc, E * TB * B + OB)
                else:
                    pe.wait_ge(a_evac, 6 * p - 2)
                for k in range(KB):
                    for u in range(2):
                        mm = pe.transpose(ps[:, 4 + k // 2, ((k % 2) * 2 + u) * P:((k % 2) * 2 + u + 1) * P],
                                          stage3[:, u, k * P:(k + 1) * P], ident[:])
                    if k % 2:
                        mm.then_inc(a_T, 1)

            def a_projections(p, first=False):
                pe.wait_ge(a_Thi, 2 * p + 2)
                pe.wait_ge(a_Tlo, 2 * p + 2)
                for job in range(6):
                    u, j = job // 3, job % 3
                    if first:
                        if u == 0:
                            pe.wait_ge(a_whi, KB * (j + 1))
                            pe.wait_ge(a_wlo, KB * (j + 1))
                        if job >= 4:
                            pe.wait_ge(a_evac, job - 3)
                    elif job < 2:
                        pe.wait_ge(a_evac, 6 * p + (job - 1))
                    elif job >= 4:
                        pe.wait_ge(a_evac, 6 * p + (job - 3))
                    for k in range(KB):
                        mm = split3(ps[:, PROJ_BANK[job]], xt3[:, 0, k, u * P:(u + 1) * P],
                                    xt3[:, 1, k, u * P:(u + 1) * P], wqkv[:, j, 0, k], wqkv[:, j, 1, k],
                                    k == 0, k == KB - 1)
                    mm.then_inc(a_proj, 1)

            def a_scores(p):
                pe.wait_ge(a_qk, 4 * p + 4)
                pe.wait_ge(a_ctx, 2 * p)
                pe.sem_inc(s_settled, 1)
                for step in range(4):
                    for i in range(16):
                        for g in range(G):
                            bank = (g + step) % 4
                            u, tok, rows = bank // 2, (bank % 2) * 16 + i, slice(32 * g, 32 * g + DH)
                            mm = pe.matmul(ps[32 * g:32 * g + 32, bank, i * H:(i + 1) * H],
                                           qT[rows, u, :, tok], kT[rows, u, :, tok], start=True, stop=True)
                mm.then_inc(a_S, 1)

            def a_context(p):
                pe.wait_ge(a_PT, 2 * p + 2)
                pe.wait_ge(a_vT, 2 * p + 2)
                pe.sem_inc(s_settled, 1)
                for step in range(4):
                    for i in range(16):
                        for g in range(G):
                            bank = (g + step) % 4
                            u, tok, rows = bank // 2, (bank % 2) * 16 + i, slice(32 * g, 32 * g + 32)
                            mm = pe.matmul(ps[rows, bank, i * (DH + 1):(i + 1) * (DH + 1)],
                                           pT[rows, u, tok, :], vT[rows, u, :, tok], start=True, stop=True)
                mm.then_inc(a_PV, 1)

            a_transposes(0, first=True)
            a_projections(0, first=True)
            with pe.Fori(0, NP2 - 1) as p:
                a_transposes(p + 1)
                a_scores(p)
                a_projections(p + 1)
                a_context(p)
            a_scores(NP2 - 1)

            def p_transposes(c, banks):
                pe.wait_ge(p_stage, 16 * c + 16)
                for k in range(KB):
                    if banks is LOOP_BANKS:
                        if k < 2:
                            pe.wait_ge(p_relu, NU * c - (1 - k))
                        else:
                            pe.wait_ge(p_Llo, NL * c - (3 - k))
                    for t in range(TB):
                        mm = pe.transpose(ps[:, banks[k], t * P:(t + 1) * P], stage4[:, t, k * P:(k + 1) * P], ident[:])
                    mm.then_inc(p_T, 1)

            def p_gate(c):
                pe.wait_ge(p_Thi, KB * c + KB)
                pe.wait_ge(p_Tlo, KB * c + KB)
                pe.wait_ge(p_top, c)
                for k in range(KB):
                    mm = split3(ps[:, 7, :], g8p[:, 0, k], g8p[:, 1, k], xth[:, 0, k], xth[:, 1, k],
                                k == 0, k == KB - 1)
                mm.then_inc(p_gps, 1)

            def p_up(c, i):
                if i == 0:
                    pe.wait_ge(p_Tlo, KB * c + KB)
                if i >= 4:
                    pe.wait_ge(p_relu, NU * c + (i - 3))
                for k in range(KB):
                    mm = split3(ps[:, i % 4, :], wup[:, 0, k, i * P:(i + 1) * P], wup[:, 1, k, i * P:(i + 1) * P],
                                xth[:, 0, k], xth[:, 1, k], k == 0, k == KB - 1)
                mm.then_inc(p_U, 1)

            def p_latent(c, b):
                pe.wait_ge(p_relu, NU * c + (5 + b))
                for k in range(KB):
                    mm = split3(ps[:, b, :], wf1[:, 0, k, b * P:(b + 1) * P], wf1[:, 1, k, b * P:(b + 1) * P],
                                xth[:, 0, k], xth[:, 1, k], k == 0, k == KB - 1)
                mm.then_inc(p_L, 1)

            def p_down(c, t):
                tok = slice(t * P, (t + 1) * P)
                if t == 0:
                    pe.wait_ge(p_Lhi, NL * c + NL)
                    pe.wait_ge(p_Llo, NL * c + NL)
                pe.wait_ge(p_Radd, TB * c + t)
                for k in range(NL):
                    mm = split3(ps[:, 6, :], lat[:, 0, k, tok], lat[:, 1, k, tok], wef[:, 0, k], wef[:, 1, k],
                                k == 0, k == NL - 1)
                mm.then_inc(p_R, 1)
                if t == 0:
                    pe.wait_ge(p_hi, NU * c + NU)
                    pe.wait_ge(p_lo, NU * c + NU)
                pe.wait_ge(p_Dadd, TB * c + (t + 1))
                for k in range(NU):
                    mm = split3(ps[:, 4 + t % 2, :], hh[:, k, 0, tok], hh[:, k, 1, tok], wdn[:, 0, k], wdn[:, 1, k],
                                k == 0, k == NU - 1)
                mm.then_inc(p_D, 1)

            def p_chunk(c, more):
                for i in range(4):
                    p_up(c, i)
                pe.wait_ge(p_rows, c + 1)
                pe.sem_inc(s_settled, 1)
                for t in range(TB):
                    mm = pe.matmul(ps[:, 7, NE * t:NE * t + NE], rows8[:, t * P:(t + 1) * P], ident[0:NE, 0:NE],
                                   start=True, stop=True)
                mm.then_inc(p_lps, 1)
                for i in range(4, NU):
                    p_up(c, i)
                for b in range(NL):
                    p_latent(c, b)
                if more:
                    p_transposes(c + 1, LOOP_BANKS)
                p_down(c, 0)
                p_down(c, 1)
                if more:
                    p_gate(c + 1)
                p_down(c, 2)
                p_down(c, 3)

            LOOP_BANKS, FIRST_BANKS = (2, 3, 0, 1), (4, 5, 7, 6)
            pe.wait_ge(p_raws, 64)
            pe.wait_ge(a_evac, 6 * NP2)
            for m in range(NL):
                for l in range(NL):
                    mm = pe.transpose(ps[:, 6, m * LAT + l * P:m * LAT + (l + 1) * P],
                                      rawe[:, l, m * P:(m + 1) * P], ident[:])
            mm.then_inc(p_eTps, 1)
            pe.wait_ge(p_eT, 1)
            for l in range(NL):
                for m in range(NL):
                    mm = pe.matmul(ps[:, 7 - l, :], expT[:, m, l * P:(l + 1) * P], raw2[:, m],
                                   start=(m == 0), stop=(m == NL - 1))
                mm.then_inc(p_ef, 1)
            pe.wait_ge(p_eflo, NL)
            p_transposes(0, FIRST_BANKS)
            a_context(NP2 - 1)
            pe.wait_ge(p_g8, 1)
            pe.wait_ge(p_wlo, 1 + KB)
            p_gate(0)
            pe.wait_ge(a_ctx, 2 * NP2)
            pe.wait_ge(p_wlo, 1 + KB + NU // 2)
            with pe.Fori(0, B - 1) as c:
                p_chunk(c, True)
            p_chunk(B - 1, False)

        @block.scalar
        def _(act):
            ch = Chain(act, s_ach)
            for job in range(0, NT, 2):
                n, lb = job // KB, job % KB
                act.wait_ge(s_xt_ps, job + 1)
                act.copy(xT[:, lb, n, :], ps[:, job % 8, :]).then_inc(s_xt_a, 1)
            for lb in range(KB):
                for n in range(B):
                    job = KB * n + lb
                    act.wait_ge(*((s_xt_a, job // 2 + 1) if job % 2 == 0 else (s_xt_v, job // 2 + 1)))
                    ins = act.activation(dump2[:], xT[:, lb, n, :], ACT.Square,
                                         accum_out=sc[:, lb, n, n:n + 1])
                    if (lb, n) == (KB - 1, B - 1):
                        ins.then_inc(s_sq, 1)
                    else:
                        ch.link(ins)
            act.wait_ge(s_pexp_in, 1)
            act.activation(sc[:, :, :, :], sc[:, :, :, :], ACT.Exp, scale=float(D) ** -0.5).then_inc(s_pexp, 1)
            act.wait_ge(s_mixw, 1)

            def copy_back(lb):
                for n in range(B):
                    act.wait_ge(s_yt, B * lb + n + 1)
                    act.copy(xs[:, TB * n:TB * n + TB, lb * P:(lb + 1) * P],
                             ps[:, (lb * B + n) % 8, :].rearrange("p (t c) -> p t c", c=P)).then_inc(s_ycp, 1)

            for lb in range(KB):
                for n in range(B):
                    if lb >= 2:
                        act.wait_ge(s_yt, B * (lb - 2) + n + 1)
                    act.activation(yT[:, lb % 2, n, :], xT[:, lb, 0, :], ACT.Copy,
                                   scale=sc[:, lb, n, 0:1]).then_inc(s_y0, 1)
                if lb >= 1:
                    copy_back(lb - 1)
            copy_back(KB - 1)
            for q in range(len(WB)):
                j, e = WB[q]
                act.wait_ge(s_raw[q % 2], 16 * (q // 2 + 1))
                act.copy(wf[:, j, e, 0], raw[:, q % 2]).then_inc(s_whi, 1)
            act.wait_ge(s_ln1, 1)
            for j in range(NT):
                act.activation(xs[:, j], xs[:, j], ACT.Identity, bias=nm[:, j:j + 1],
                               scale=rs[:, j:j + 1]).then_inc(s_x1, 1)

            def m_prep(c, last_F):
                for k in range(KB):
                    act.wait_ge(m_T, KB * c + (k + 1))
                    if k == 0:
                        act.wait_ge(m_F, last_F)
                    act.copy(xth[:, 0, k], ps[:, k, :]).then_inc(m_Thi, 1)
                act.wait_ge(m_stage, 16 * c + 16)
                for t in range(TB):
                    ins = act.activation(stage[:, t], stage[:, t], ACT.Abs, accum_out=absum[:, t:t + 1])
                    if t < TB - 1:
                        ch.link(ins)
                    else:
                        ins.then_inc(m_abs, 1)

            def m_rowcopy(c):
                act.wait_ge(m_gps, c + 1)
                act.wait_ge(m_gbias, c + 1)
                act.activation(rowsE[:], ps[0:E, 7, :], ACT.Identity, bias=gbias[0:E]).then_inc(m_rows, 1)

            def m_act(c, e, f):
                j = e * KB + f
                if f == 0:
                    act.wait_ge(m_O, E * TB * c + (TB if e == 2 else 0))
                act.wait_ge(m_F, E * KB * c + (j + 1))
                act.wait_ge(m_lo, E * KB * c + (j + 1))
                act.activation(act32[:, j % 2], ps[:, f, :], FUNCS[e], bias=b1c[:, e, f:f + 1]).then_inc(m_A, 1)
                act.activation(a2[:, e % 2, 0, f], ps[:, f, :], FUNCS[e], bias=b1c[:, e, f:f + 1]).then_inc(m_hi, 1)

            def m_chunk(c, more):
                for f in range(KB):
                    m_act(c, 0, f)
                act.wait_ge(m_shift, c + 1)
                act.activation(pr, pr, ACT.Exp).then_inc(m_exp, 1)
                for f in range(KB):
                    m_act(c, 1, f)
                act.wait_ge(m_cTps, c + 1)
                act.copy(rowsE[:], ps[0:E, 7, :]).then_inc(m_cT, 1)
                for f in range(KB):
                    m_act(c, 2, f)
                if more:
                    m_prep(c + 1, E * KB * c + E * KB)
                    m_rowcopy(c + 1)
                else:
                    for jk in range(3 * KB):
                        j, k = jk // KB, jk % KB
                        act.wait_ge(a_wps, jk + 1)
                        if jk == 0:
                            act.wait_ge(m_F, E * KB * B)
                        elif k == 0:
                            act.wait_ge(m_O, E * TB * C3 + j * TB)
                        act.copy(wqkv[:, j, 0, k], ps[:, k, :]).then_inc(a_whi, 1)

            m_prep(0, 0)
            act.wait_ge(m_gwp, 1)
            m_rowcopy(0)
            C3 = B - 1
            with act.Fori(0, B - 1) as c:
                m_chunk(c, True)
            m_chunk(B - 1, False)

            def a_highs(p):
                for h in range(2):
                    act.wait_ge(a_T, 2 * p + (h + 1))
                    if h == 0:
                        act.wait_ge(a_proj, 6 * p)
                    act.copy(xt3[:, 0, 2 * h:2 * h + 2], ps[:, 4 + h, :].rearrange("p (k t) -> p k t", k=2)
                             ).then_inc(a_Thi, 1)

            def a_exps(p):
                for u in range(2):
                    act.wait_ge(a_shift, 2 * p + (u + 1))
                    act.activation(sh[:, u], sh[:, u], ACT.Exp, scale=DH ** -0.5).then_inc(a_exp, 1)

            a_highs(0)
            with act.Fori(0, NP2 - 1) as p:
                a_highs(p + 1)
                a_exps(p)

            act.wait_ge(p_raws, 64)
            act.copy(wf1[:, 0], raw1[:]).then_inc(p_whi, 1)
            act.wait_ge(p_rawu, 16)
            act.wait_ge(a_proj, 6 * NP2)
            for k in range(KB):
                act.copy(wup[:, 0, k], rawu[:, k]).then_inc(p_whi, 1)
            a_exps(NP2 - 1)
            act.wait_ge(p_eTps, 1)
            act.copy(expT[:], ps[:, 6, :].rearrange("p (m l) -> p m l", m=NL)).then_inc(p_eT, 1)
            for l in range(NL):
                act.wait_ge(p_ef, l + 1)
                act.copy(wef[:, 0, l], ps[:, 7 - l, :]).then_inc(p_efhi, 1)

            def p_highs(c, banks):
                for k in range(KB):
                    act.wait_ge(p_T, KB * c + (k + 1))
                    if k == 0:
                        act.wait_ge(p_L, NL * c)
                    act.copy(xth[:, 0, k], ps[:, banks[k], :]).then_inc(p_Thi, 1)

            def p_rowcopy(c):
                act.wait_ge(p_gps, c + 1)
                act.copy(rows8[:], ps[0:NE, 7, :]).then_inc(p_rows, 1)

            def p_square(c, i):
                act.wait_ge(p_U, NU * c + (i + 1))
                act.wait_ge(p_lo, NU * c + (i - 1) if i >= 2 else NU * c)
                act.activation(relu[i % 2][:], ps[:, i % 4, :], ACT.Relu).then_inc(p_relu, 1)
                act.wait_ge(p_relu, NU * c + (i + 1))
                if i == 0:
                    act.wait_ge(p_D, TB * c)
                act.activation(hh[:, i, 0], relu[i % 2][:], ACT.Square).then_inc(p_hi, 1)

            def p_chunk(c, more):
                for i in range(NU):
                    p_square(c, i)
                for b in range(NL):
                    act.wait_ge(p_L, NL * c + (b + 1))
                    act.wait_ge(p_R, TB * c)
                    act.copy(lat[:, 0, b], ps[:, b, :]).then_inc(p_Lhi, 1)
                if more:
                    p_highs(c + 1, LOOP_BANKS)
                    p_rowcopy(c + 1)

            LOOP_BANKS, FIRST_BANKS = (2, 3, 0, 1), (4, 5, 7, 6)
            act.wait_ge(p_ef, NL)
            act.wait_ge(a_proj, 6 * NP2)
            p_highs(0, FIRST_BANKS)
            act.wait_ge(a_PV, NP2)
            act.wait_ge(p_rawd, 16)
            act.wait_ge(p_wlo, 1 + KB)
            for k in range(0, NU, 2):
                act.copy(wdn[:, 0, k:k + 2], rawd[:, k:k + 2]).then_inc(p_whi, 1)
            act.wait_ge(p_wlo, 1 + KB + NU // 2)
            p_rowcopy(0)
            act.wait_ge(a_qk, 4 * NP2)
            act.wait_ge(a_ctx, 2 * NP2)
            with act.Fori(0, B - 1) as c:
                p_chunk(c, True)
            p_chunk(B - 1, False)

        @block.vector
        def _(dve):
            ch = Chain(dve, s_vch)
            M_LINKS, A_LINKS, P_LINKS = 51, 27, 97

            def rsqrt(n):
                v, m = mv[:, 0:n, 1], mv[:, 0:n, 0]
                r, h, t = rs[:, 0:n], hv[:, 0:n], nm[:, 0:n]
                ch.link(dve.tensor_scalar(h, v, EPS, None, ALU.add))
                ch.link(dve.tensor_scalar(t.bitcast(I32), h.bitcast(I32), 1, None, ALU.arith_shift_right))
                ch.link(dve.tensor_scalar(t.bitcast(I32), t.bitcast(I32), -1, None, ALU.bitwise_xor))
                dve.sem_inc(s_settled, 1)
                ch.link(dve.tensor_tensor(r.bitcast(I32), t.bitcast(I32), magic[:, 0:1].broadcast_to([P, n]), ALU.add))
                ch.link(dve.tensor_scalar(h, h, -0.5, None, ALU.mult))
                for _ in range(3):
                    ch.link(dve.tensor_tensor(t, r, r, ALU.mult))
                    ch.link(dve.tensor_tensor(t, t, h, ALU.mult))
                    ch.link(dve.scalar_tensor_tensor(out=r, in0=t, scalar=1.5, in1=r, op0=ALU.add, op1=ALU.mult))
                return dve.scalar_tensor_tensor(out=t, in0=m, scalar=-1.0, in1=r, op0=ALU.mult, op1=ALU.mult)

            ch.link(dve.memset(magic, RSQRT_MAGIC + 1))
            for job in range(1, NT, 2):
                n, lb = job // KB, job % KB
                dve.wait_ge(s_xt_ps, job + 1)
                dve.tensor_copy(xT[:, lb, n, :], ps[:, job % 8, :]).then_inc(s_xt_v, 1)
            dve.wait_ge(s_xt_a, NT // 2)
            dve.wait_ge(s_xt_v, NT // 2)
            for lb in range(KB):
                for n in range(B):
                    for m in range(n + 1, B):
                        ch.link(dve.tensor_tensor_reduce(dump[:], xT[:, lb, n, :], xT[:, lb, m, :], 1.0, 0.0,
                                                         ALU.mult, ALU.add, sc[:, lb, n, m:m + 1]))
            for n in range(B):
                for m in range(n + 1, B):
                    ch.link(dve.tensor_copy(sc[:, :, m, n], sc[:, :, n, m]))
            dve.wait_ge(s_sq, 1)
            sc3 = small[:, 0:64].rearrange("p (r m) -> p r m", m=B)
            ch.link(dve.tensor_reduce(mx, sc3, X, ALU.max))
            dve.tensor_tensor(sc3, sc3, mx.unsqueeze(2).broadcast_to([P, KB * B, B]),
                              ALU.subtract).then_inc(s_pexp_in, 1)
            dve.wait_ge(s_pexp, 1)
            ch.link(dve.tensor_reduce(mx, sc3, X, ALU.add))
            ch.link(dve.reciprocal(mx, mx))
            ch.link(dve.tensor_tensor(sc3, sc3, mx.unsqueeze(2).broadcast_to([P, KB * B, B]), ALU.mult))
            for n in range(B):
                ins = dve.tensor_scalar(sc[:, :, n, n], sc[:, :, n, n], 2.0, None, ALU.add)
                if n < B - 1:
                    ch.link(ins)
                else:
                    ins.then_inc(s_mixw, 1)
            dve.wait_ge(s_mixw, 1)
            for lb in range(KB):
                for n in range(B):
                    dve.wait_ge(s_y0, B * lb + n + 1)
                    for m in range(1, B):
                        ins = dve.scalar_tensor_tensor(out=yT[:, lb % 2, n, :], in0=xT[:, lb, m, :],
                                                       scalar=sc[:, lb, n, m:m + 1], in1=yT[:, lb % 2, n, :],
                                                       op0=ALU.mult, op1=ALU.add)
                        if m < B - 1:
                            ch.link(ins)
                        else:
                            ins.then_inc(s_y, 1)
            dve.wait_ge(s_ycp, KB * B)
            for j in range(NT):
                ch.link(dve.bn_stats(stats, xs[:, j]))
                ch.link(dve.bn_aggr(mv[:, j], stats))
            rsqrt(NT).then_inc(s_ln1, 1)

            def m_lows(c):
                for k in range(KB):
                    dve.wait_ge(m_Thi, KB * c + (k + 1))
                    dve.tensor_tensor(xth[:, 1, k], ps[:, k, :], xth[:, 0, k].bitcast(F32),
                                      ALU.subtract).then_inc(m_Tlo, 1)
                dve.wait_ge(m_abs, c + 1)
                dve.tensor_tensor(statin, absum.unsqueeze(2).broadcast_to([P, TB, 2]), vmask,
                                  ALU.mult).then_inc(m_stat, 1)

            def m_ratio(c):
                dve.wait_ge(m_statps, c + 1)
                ch.link(dve.tensor_copy(ratio[:, 0:2], ps[:, 7, 0:2]))
                ch.link(dve.tensor_scalar(ratio[:, 1:2], ratio[:, 1:2], 1e-8, None, ALU.add))
                ch.link(dve.reciprocal(ratio[:, 1:2], ratio[:, 1:2]))
                ch.link(dve.tensor_tensor(ratio[:, 2:3], ratio[:, 0:1], ratio[:, 1:2], ALU.mult))
                dve.scalar_tensor_tensor(out=gbias[0:E], in0=gw_last[0:E], scalar=ratio[0:E, 2:3],
                                         in1=gb_col[0:E], op0=ALU.mult, op1=ALU.add).then_inc(m_gbias, 1)

            def m_route(c):
                over = tA.unsqueeze(2).broadcast_to([P, TB, E])
                dve.wait_ge(m_lps, c + 1)
                ch.link(dve.tensor_copy(pr, ps[:, 7, 0:4 * TB].rearrange("p (t e) -> p t e", e=4)[:, :, 0:E]))
                ch.link(dve.tensor_reduce(tA, pr, X, ALU.max))
                dve.tensor_tensor(pr, pr, over, ALU.subtract).then_inc(m_shift, 1)
                dve.wait_ge(m_exp, c + 1)
                ch.link(dve.tensor_reduce(tA, pr, X, ALU.add))
                ch.link(dve.reciprocal(tA, tA))
                dve.tensor_tensor(pr, pr, over, ALU.mult).then_inc(m_prob, 1)
                dve.wait_ge(m_prob, c + 1)
                ch.link(dve.tensor_reduce(top[:, 0], pr, X, ALU.max))
                ch.link(dve.tensor_tensor(tA, pr[:, :, 0], pr[:, :, 1], ALU.min))
                ch.link(dve.tensor_tensor(tB, pr[:, :, 0], pr[:, :, 1], ALU.max))
                ch.link(dve.tensor_tensor(tB, tB, pr[:, :, 2], ALU.min))
                ch.link(dve.tensor_tensor(top[:, 1], tA, tB, ALU.max))
                ch.link(dve.scalar_tensor_tensor(out=tA, in0=top[:, 0], scalar=1e-8, in1=top[:, 1],
                                                 op0=ALU.add, op1=ALU.add))
                ch.link(dve.reciprocal(tA, tA))
                ch.link(dve.tensor_tensor(top, top, tA.unsqueeze(1).broadcast_to([P, 2, TB]), ALU.mult))
                dve.wait_ge(m_t0, c + 1)
                ch.link(dve.tensor_copy(rank, ps[:, 7, 0:E]))
                ch.link(dve.tensor_tensor(cmp3[:, 0:1], rank[:, 0:1], rank[:, 1:2], ALU.is_ge))
                ch.link(dve.tensor_tensor(cmp3[:, 1:2], rank[:, 0:1], rank[:, 2:3], ALU.is_ge))
                ch.link(dve.tensor_tensor(cmp3[:, 2:3], rank[:, 1:2], rank[:, 2:3], ALU.is_ge))
                ch.link(dve.tensor_tensor(rank[:, 0:1], cmp3[:, 0:1], cmp3[:, 1:2], ALU.add))
                ch.link(dve.tensor_scalar(rank[:, 0:1], rank[:, 0:1], -1.0, 2.0, ALU.mult, ALU.add))
                ch.link(dve.scalar_tensor_tensor(out=rank[:, 1:2], in0=cmp3[:, 0:1], scalar=1.0, in1=cmp3[:, 2:3],
                                                 op0=ALU.add, op1=ALU.subtract))
                ch.link(dve.tensor_tensor(rank[:, 2:3], cmp3[:, 1:2], cmp3[:, 2:3], ALU.add))
                ch.link(dve.tensor_scalar(sel[:, 0], rank, 0.0, None, ALU.is_equal))
                ch.link(dve.tensor_scalar(sel[:, 1], rank, 1.0, None, ALU.is_equal))
                for i, dst in ((0, coef), (1, tmp)):
                    ch.link(dve.tensor_tensor(dst, top[:, i].unsqueeze(2).broadcast_to([P, TB, E]),
                                              sel[:, i].unsqueeze(1).broadcast_to([P, TB, E]), ALU.mult))
                dve.tensor_tensor(coef, coef, tmp, ALU.add).then_inc(m_coef, 1)

            def m_add(c, e, t):
                j = e * TB + t
                dve.wait_ge(m_O, E * TB * c + (j + 1))
                dve.scalar_tensor_tensor(out=acc[:, t], in0=ps[:, 4 + j % OB, :], scalar=coef[:, t, e:e + 1],
                                         in1=acc[:, t], op0=ALU.mult, op1=ALU.add).then_inc(m_Oacc, 1)

            def m_chunk(c, more):
                m_route(c)
                dve.wait_ge(m_coef, c + 1)
                for t in range(TB):
                    dve.wait_ge(m_bc, TB * c + (t + 1))
                    dve.tensor_tensor(acc[:, t], ps[:, 7, :], xs[:, TB * c + t], ALU.add).then_inc(m_acc0, 1)
                    dve.wait_ge(m_acc0, TB * c + (t + 1))
                    m_add(c, 0, t)
                if more:
                    m_lows(c + 1)
                else:
                    a_weight_lows(0)
                dve.wait_ge(m_Oacc, E * TB * c + (TB + OB))
                m_add(c, 1, 0)
                m_add(c, 1, 1)
                if more:
                    m_ratio(c + 1)
                else:
                    a_weight_lows(1)
                m_add(c, 1, 2)
                m_add(c, 1, 3)
                if not more:
                    a_weight_lows(2)
                dve.wait_ge(m_Oacc, E * TB * c + (2 * TB + OB))
                for t in range(TB):
                    m_add(c, 2, t)
                    dve.wait_ge(m_Oacc, E * TB * c + (2 * TB + OB + t + 1))
                    ch.link(dve.bn_stats(stats4[:, t], acc[:, t]))
                    dve.sem_inc(s_settled, 1)
                    ch.link(dve.bn_aggr(mv[:, t], stats4[:, t]))
                ch.link(rsqrt(TB))
                for t in range(TB):
                    dve.tensor_scalar(xs[:, TB * c + t], acc[:, t], rs[:, t:t + 1], nm[:, t:t + 1],
                                      ALU.mult, ALU.add).then_inc(m_x2, 1)

            def a_weight_lows(j):
                for k in range(KB):
                    dve.wait_ge(a_whi, KB * j + k + 1)
                    dve.tensor_tensor(wqkv[:, j, 1, k], ps[:, k, :], wqkv[:, j, 0, k].bitcast(F32),
                                      ALU.subtract).then_inc(a_wlo, 1)

            dve.wait_ge(s_x1, NT)
            dve.wait_ge(m_gwp, 1)
            ch.link(dve.memset(tA, 0.0))
            dve.memset(tA, 0.0).then_inc(m_Oacc, OB)
            m_lows(0)
            m_ratio(0)
            ch.end()
            with dve.Fori(0, B - 1) as c:
                ch.begin(c, M_LINKS)
                m_chunk(c, True)
            ch.end(B - 1)
            m_chunk(B - 1, False)
            ch.end()

            def a_lows(p):
                for h in range(2):
                    dve.wait_ge(a_Thi, 2 * p + (h + 1))
                    dve.tensor_tensor(xt3[:, 1, 2 * h:2 * h + 2], ps[:, 4 + h, :].rearrange("p (k t) -> p k t", k=2),
                                      xt3[:, 0, 2 * h:2 * h + 2].bitcast(F32), ALU.subtract).then_inc(a_Tlo, 1)

            def a_softmax_shift(p, u):
                rows = ps[:, 2 * u:2 * u + 2, :].rearrange("p b (i t) -> p (b i) t", t=H)
                ch.link(dve.tensor_reduce(mx3[:, u], rows, X, ALU.max))
                dve.tensor_tensor(sh[:, u], rows, mx3[:, u].unsqueeze(2).broadcast_to([P, 32, H]),
                                  ALU.subtract).then_inc(a_shift, 1)

            def overlapped(t, u):
                return bass.AP(tensor=t[:].tensor, offset=u * (D + DH), ap=[[2 * (D + DH), P], [DH, H], [1, 32]])

            def a_copy(p, job):
                u, j = job // 3, job % 3
                dst, bias = ((qs, bq_b), (ks, bk_b), (vs, bv_b))[j]
                dve.wait_ge(a_proj, 6 * p + (job + 1))
                dve.tensor_tensor(dst[:, u, 0:D], ps[:, PROJ_BANK[job], :], bias[:], ALU.add).then_inc(a_evac, 1)
                if j < 2:
                    dve.wait_ge(a_evac, 6 * p + (job + 1))
                    dve.transpose((qT, kT)[j][:, u], overlapped(dst, u)).then_inc(a_qk, 1)

            def a_turn_v(p, u):
                dve.wait_ge(a_evac, 6 * p + 6)
                dve.transpose(vT[:, u, 0:DH], vs[:, u].rearrange("p (t d) -> p d t", d=DH)).then_inc(a_vT, 1)

            def a_turn_probs(p, u):
                dve.wait_ge(a_exp, 2 * p + (u + 1))
                dve.transpose(pT[:, u], sh[:, u]).then_inc(a_PT, 1)

            def a_finish(p):
                dve.wait_ge(a_PV, p + 1)
                for u in range(2):
                    got = ps[:, 2 * u:2 * u + 2, 0:16 * (DH + 1)].rearrange("p b (i d) -> p b i d", d=DH + 1)
                    inv = mx3[:, u].rearrange("p (b i) -> p b i", b=2)
                    ch.link(dve.reciprocal(inv, got[:, :, :, DH]))
                    dve.tensor_tensor(ctxs[:, u].rearrange("p (b i) d -> p b i d", b=2), got[:, :, :, 0:DH],
                                      inv.unsqueeze(3).broadcast_to([P, 2, 16, DH]), ALU.mult).then_inc(a_ctx, 1)
                    dve.wait_ge(a_ctx, 2 * p + (u + 1))
                    ch.link(dve.transpose(attn[:, u].rearrange("p (h d) -> p d h", d=DH),
                                          ctxs[:, u].rearrange("p i d -> p d i")))
                    ch.link(dve.tensor_tensor(acc3[:, u], attn[:, u], xs[:, 2 * p + u], ALU.add))
                    ch.link(dve.bn_stats(stats4[:, u], acc3[:, u]))
                    dve.sem_inc(s_settled, 1)
                    ch.link(dve.bn_aggr(mv[:, u], stats4[:, u]))
                ch.link(rsqrt(2))
                for u in range(2):
                    dve.tensor_scalar(xs[:, 2 * p + u], acc3[:, u], rs[:, u:u + 1], nm[:, u:u + 1],
                                      ALU.mult, ALU.add).then_inc(a_x3, 1)

            def a_pair(p, more):
                if more:
                    a_lows(p + 1)
                dve.wait_ge(a_S, p + 1)
                a_softmax_shift(p, 0)
                a_softmax_shift(p, 1)
                if more:
                    a_copy(p + 1, 0)
                    a_copy(p + 1, 1)
                a_turn_probs(p, 0)
                a_turn_probs(p, 1)
                if more:
                    for job in range(2, 6):
                        a_copy(p + 1, job)
                else:
                    p_first_lows()
                a_finish(p)
                if more:
                    a_turn_v(p + 1, 0)
                    a_turn_v(p + 1, 1)

            def p_lows(c, banks):
                for k in range(KB):
                    dve.wait_ge(p_Thi, KB * c + (k + 1))
                    dve.tensor_tensor(xth[:, 1, k], ps[:, banks[k], :], xth[:, 0, k].bitcast(F32),
                                      ALU.subtract).then_inc(p_Tlo, 1)

            def p_first_lows():
                for l in range(NL):
                    dve.wait_ge(p_efhi, l + 1)
                    dve.tensor_tensor(wef[:, 1, l], ps[:, 7 - l, :], wef[:, 0, l].bitcast(F32),
                                      ALU.subtract).then_inc(p_eflo, 1)
                dve.wait_ge(a_vT, 2 * NP2)
                p_lows(0, FIRST_BANKS)

            LOOP_BANKS, FIRST_BANKS = (2, 3, 0, 1), (4, 5, 7, 6)
            dve.wait_ge(m_x2, NT)
            dve.wait_ge(a_bias, 48)
            dve.wait_ge(a_const, 3)
            a_lows(0)
            for job in range(6):
                a_copy(0, job)
            a_turn_v(0, 0)
            a_turn_v(0, 1)
            ch.end()
            with dve.Fori(0, NP2 - 1) as p:
                ch.begin(p, A_LINKS)
                a_pair(p, True)
            ch.end(NP2 - 1)
            a_pair(NP2 - 1, False)
            ch.end()

            def p_square_low(c, i):
                dve.wait_ge(p_hi, NU * c + (i + 1))
                dve.wait_ge(p_lo, NU * c + i)
                ch.link(dve.tensor_tensor(sq32[:], relu[i % 2][:], relu[i % 2][:], ALU.mult))
                dve.tensor_tensor(hh[:, i, 1], sq32[:], hh[:, i, 0].bitcast(F32), ALU.subtract).then_inc(p_lo, 1)

            def p_route(c):
                dve.wait_ge(p_lps, c + 1)
                dve.tensor_copy(logit8, ps[:, 7, 0:TB * NE].rearrange("p (t e) -> p t e", e=NE)).then_inc(p_top, 1)
                dve.wait_ge(p_top, c + 1)
                for t in range(TB):
                    dve.sem_inc(s_settled, 1)
                    ch.link(dve.max(top8[:, t], logit8[:, t]))
                ch.link(dve.tensor_tensor(route, top8[:, :, 0], top8[:, :, 1], ALU.add))

            def p_statistics(t):
                ch.link(dve.bn_stats(stats4[:, t % 2], acc4[:, t]))
                dve.sem_inc(s_settled, 1)
                ch.link(dve.bn_aggr(mv[:, t % 2], stats4[:, t % 2]))

            def p_norms(c, t0):
                ch.link(rsqrt(2))
                for u in range(2):
                    y = acc4[:, t0 + u]
                    ch.link(dve.scalar_tensor_tensor(out=y, in0=y, scalar=mv[:, u, 0:1], in1=gam_b[:],
                                                     op0=ALU.subtract, op1=ALU.mult))
                    dve.wait_ge(p_xb, TB * c + (t0 + u + 1))
                    ch.link(dve.scalar_tensor_tensor(out=y, in0=y, scalar=rs[:, u:u + 1], in1=xs[:, TB * c + t0 + u],
                                                     op0=ALU.mult, op1=ALU.add))
                for u in range(2):
                    p_statistics(t0 + u)
                ch.link(rsqrt(2))
                for u in range(2):
                    dve.tensor_scalar(acc4[:, t0 + u], acc4[:, t0 + u], rs[:, u:u + 1], nm[:, u:u + 1],
                                      ALU.mult, ALU.add).then_inc(p_y, 1)

            def p_chunk(c, more):
                for i in range(4):
                    p_square_low(c, i)
                p_route(c)
                for i in range(4, NU):
                    p_square_low(c, i)
                for b in range(NL):
                    dve.wait_ge(p_Lhi, NL * c + (b + 1))
                    dve.tensor_tensor(lat[:, 1, b], ps[:, b, :], lat[:, 0, b].bitcast(F32),
                                      ALU.subtract).then_inc(p_Llo, 1)
                if more:
                    p_lows(c + 1, LOOP_BANKS)
                dve.wait_ge(s_out, 16 * TB * c)
                for t in range(TB):
                    dve.wait_ge(p_R, TB * c + (t + 1))
                    dve.tensor_scalar(acc4[:, t], ps[:, 6, :], route[:, t:t + 1], None,
                                      ALU.mult).then_inc(p_Radd, 1)
                    dve.wait_ge(p_Radd, TB * c + (t + 1))
                    dve.wait_ge(p_D, TB * c + (t + 1))
                    dve.tensor_tensor(acc4[:, t], acc4[:, t], ps[:, 4 + t % 2, :], ALU.add).then_inc(p_Dadd, 1)
                    dve.wait_ge(p_Dadd, TB * c + (t + 3))
                    p_statistics(t)
                    if t % 2:
                        p_norms(c, t - 1)

            dve.wait_ge(a_x3, NT)
            ch.link(dve.memset(tB, 0.0))
            dve.memset(tB, 0.0).then_inc(p_Dadd, 2)
            ch.end()
            with dve.Fori(0, B - 1) as c:
                ch.begin(c, P_LINKS)
                p_chunk(c, True)
            ch.end(B - 1)
            p_chunk(B - 1, False)
            ch.end()


_INS = ['L0_attn_x', 'L0_ffn_gate_w', 'L0_ffn_gate_b', 'L0_ffn_w1', 'L0_ffn_b1', 'L0_ffn_w2', 'L0_ffn_b2',
        'L1_attn_wq', 'L1_attn_bq', 'L1_attn_wk', 'L1_attn_bk', 'L1_attn_wv', 'L1_attn_bv',
        'L1_ffn_gate_w', 'L1_ffn_up_w', 'L1_ffn_down_w', 'L1_ffn_fc1_w', 'L1_ffn_fc2_w', 'L1_ffn_expert_w',
        'L1_ffn_ln_gamma', 'L1_ffn_ln_beta']


def kernel(**inputs):
    import numpy as np
    import concourse.bacc as bacc
    from concourse.bass_utils import run_bass_kernel_spmd

    nc = bacc.Bacc("TRN2", target_bir_lowering=False, num_devices=1)
    arrays, args = {}, []
    for name in _INS:
        a = np.ascontiguousarray(inputs[name])
        arrays[f"in_{name}"] = a
        args.append(nc.dram_tensor(f"in_{name}", a.shape, mybir.dt.from_np(a.dtype), kind="ExternalInput").ap())
    out = nc.dram_tensor("out", (B, S, D), F32, kind="ExternalOutput").ap()
    build_program(nc, *args, out)
    r = run_bass_kernel_spmd(nc, [arrays], core_ids=[0])
    return r.results[0]["out"]
```

```python
from contextlib import ExitStack

import concourse.bass as bass
from concourse import mybir

F32 = mybir.dt.float32
F32R = mybir.dt.float32r
BF16 = mybir.dt.bfloat16
I32 = mybir.dt.int32
ALU = mybir.AluOpType
ACT = mybir.ActivationFunctionType
X = mybir.AxisListType.X

P = 128
B = 4
S = 512
D = 512
KB = D // P
TB = S // P
NT = B * TB
E = 3
SL = 2
H, DH = 32, 16
INT, LAT, NE = 1024, 256, 8
NU, NL = INT // P, LAT // P
VIS = int(S * 0.3)
EPS = 1e-5
RSQRT_MAGIC = 0x5F3759DF


class Chain:

    def __init__(self, eng, sem):
        self.eng, self.sem, self.base, self.i, self.per, self.k = eng, sem, 0, 0, 0, 0

    def link(self, ins):
        self.k += 1
        ins.then_inc(self.sem, 1)
        self.eng.wait_ge(self.sem, self.i * self.per + (self.base + self.k))

    def begin(self, i=0, per=0):
        self.i, self.per, self.k = i, per, 0

    def end(self, times=1):
        assert self.per in (0, self.k), f"links in the loop's body: {self.k}"
        self.base += times * self.k
        self.i = self.per = self.k = 0


def build_program(nc, x, gate_w, gate_b, w1, b1, w2, b2, wq, bq, wk, bk, wv, bv,
                  gate8_w, up_w, down_w, fc1_w, fc2_w, expert_w, gamma, beta, out):
    with ExitStack() as ctx:
        base = (nc.sbuf_base + 31) // 32 * 32
        top = nc.sbuf_usable_end

        def at(name, shape, offset, dt=F32):
            size = 2 if dt == BF16 else 4
            for n in shape[1:]:
                size *= n
            assert base + offset + size <= top, name
            return nc.alloc_sbuf_tensor_at(name, shape, dt, offset=base + offset)

        def sem(name):
            return ctx.enter_context(nc.semaphore(name))

        K = 1024
        RES = 0
        XT_AT = 32 * K
        ACT_AT = 48 * K
        W_AT = 80 * K
        MISC = 176 * K
        xs = at("xs", [P, NT, D], RES)
        xT = at("xT", [P, KB, B, S], W_AT + 64 * K)
        yT = at("yT", [P, B, KB, S], ACT_AT)
        terms = at("terms", [P, 8, S], MISC)
        dump = at("dump", [P, 2, S], MISC + 16 * K)
        wf = at("wf", [P, 2, E, 2, KB, D], W_AT, F32R)
        wraw = at("wraw", [P, 2, E, 2, KB, D], W_AT)
        stage = at("stage", [P, TB, D], MISC)
        bias_rows = at("bias_rows", [2 * 32, D], MISC + 8 * K, F32R)
        bias_high = at("bias_high", [2 * 32, D], MISC + 10 * K, F32R)
        bias_neg = at("bias_neg", [2 * 32, D], MISC + 12 * K)
        pick = at("pick", [2 * 32, E, P], MISC + 14 * K, F32R)
        act32 = at("act32", [P, 2, S], MISC + 16 * K)
        gwp = at("gwp", [P, 2, KB, P], MISC + 20 * K, F32R)
        rowsE = at("rowsE", [E, S], MISC + 24 * K)
        bias_raw = at("bias_raw", [2 * 32, D], MISC + 26 * K)
        small2 = at("small2", [P, 256], MISC + 28 * K)
        xth = at("xth", [P, 2, KB, S], XT_AT, F32R)
        a2 = at("a2", [P, 2, 2, KB, S], ACT_AT, F32R)
        rawq = at("rawq", [P, 3, KB, D], W_AT)
        wqkv = at("wqkv", [P, 3, 2, KB, D], W_AT + 32 * K, F32R)
        vT = at("vT", [P, 2, DH + 1, 32], W_AT + 24 * K)
        xt3 = at("xt3", [P, 2, KB, 2 * P], XT_AT, F32R)
        vs = at("vs", [P, 2, D], XT_AT + 8 * K)
        rest = at("rest", [P, 2, D], XT_AT + 12 * K)
        q3 = at("q3", [P, 2, 3, H // 2, DH, 2], MISC + 16 * K, BF16)
        k3 = at("k3", [P, 2, 3, H // 2, DH, 2], MISC + 22 * K, BF16)
        qT = (at("qT0", [P, 2, 32, H], MISC + 4 * K, BF16), at("qT1", [P, 2, 32, H], W_AT + 92 * K, BF16))
        kT = at("kT", [P, 2, 3, 32, H], W_AT + 80 * K, BF16)
        qdiag = at("qdiag", [P, 2, 32, P], ACT_AT, BF16)
        sh = at("sh", [P, 2, 32, H], ACT_AT + 16 * K)
        ctxs = sh[:, :, :, 0:DH]
        pT = at("pT", [P, 2, 32, H], ACT_AT + 24 * K)
        stage3 = at("stage3", [P, 2, D], MISC)
        attn = at("attn", [P, 2, D], MISC + 10 * K)
        rawu = at("rawu", [P, KB, INT], W_AT)
        raw1 = at("raw1", [P, KB, LAT], W_AT + 16 * K)
        raw2 = at("raw2", [P, NL, D], W_AT + 20 * K)
        rawe = at("rawe", [P, NL, LAT], W_AT + 29 * K)
        rawd = at("rawd", [P, NU, D], W_AT + 64 * K)
        wup = at("wup", [P, 2, KB, INT], W_AT + 32 * K, F32R)
        wdn = at("wdn", [P, 2, NU, D], W_AT, F32R)
        wf1 = at("wf1", [P, 2, KB, LAT], W_AT + 80 * K, F32R)
        wef = at("wef", [P, 2, NL, D], W_AT + 88 * K, F32R)
        lat = at("lat", [P, 2, NL, S], W_AT + 64 * K, F32R)
        gam_b = at("gam_b", [P, D], W_AT + 72 * K)
        bet_b = at("bet_b", [P, D], W_AT + 74 * K)
        rows8 = at("rows8", [NE, S], W_AT + 76 * K)
        expT = at("expT", [P, NL, LAT], XT_AT)
        hh = at("hh", [P, NU, 2, S], ACT_AT, F32R)
        stage4 = at("stage4", [P, TB, D], MISC)
        acc4 = at("acc4", [P, TB, D], MISC + 8 * K)
        relu = [at(f"relu{i}", [P, S], where) for i, where in enumerate(
            (MISC + 16 * K, MISC + 26 * K, MISC + 24 * K, W_AT + 78 * K))]
        g8p = at("g8p", [P, 2, KB, P], MISC + 18 * K, F32R)
        sq32 = at("sq32", [P, S], MISC + 22 * K)
        SM = MISC + 30 * K
        ident = at("ident", [P, P], SM)
        ones = at("ones", [P, P], SM + 512)
        small = at("small", [P, 180], SM + 1024)

        ps = ctx.enter_context(nc.psum_tensor("ps", [P, 8, 512], F32))

        s_x = [sem(f"x_block{k}_loaded") for k in range(KB)]
        s_raw = [sem(f"expert_weights{n}_loaded") for n in range(2 * E)]
        s_ident = sem("ident_written")
        s_xt_ps = sem("x_transposed_in_psum")
        s_xt = sem("xT_copied")
        s_sq = sem("squares_summed")
        s_pexp_in = sem("shifted_scores_ready")
        s_pexp = sem("score_exps_ready")
        s_mixw = sem("mix_weights_ready")
        s_y0 = sem("first_mix_term_ready")
        s_terms = sem("mix_terms_for_pool_ready")
        s_y = sem("mixed_rows_ready")
        s_y_pool = sem("mixed_rows_of_pool_ready")
        s_yt = sem("mixed_rows_transposed_in_psum")
        s_ycp = sem("mixed_rows_copied_back")
        s_x1 = sem("x1_tiles_written")
        s_whi = sem("w_high_written")
        s_wlo = sem("w_low_written")
        s_vch = sem("vector_chain")
        s_ach = sem("scalar_chain")
        s_gch = sem("pool_chain")
        s_out = sem("out_stored")
        s_settled = sem("settled")
        m_consts = sem("m_consts_loaded")
        m_gwp = sem("m_gate_weights_split")
        m_stage = sem("m_x_staged")
        m_T = sem("m_xT_in_psum")
        m_Thi = sem("m_xT_high_written")
        m_Tlo = sem("m_xT_low_written")
        m_abs = sem("m_abs_sums_ready")
        m_stat = sem("m_stat_terms_ready")
        m_statps = sem("m_stat_sums_in_psum")
        m_gbias = sem("m_gate_bias_ready")
        m_gps = sem("m_gate_rows_in_psum")
        m_rows = sem("m_logit_rows_copied")
        m_lps = sem("m_logits_in_psum")
        m_shift = sem("m_logits_shifted")
        m_exp = sem("m_exps_ready")
        m_prob = sem("m_probs_ready")
        m_t0 = sem("m_first_token_in_psum")
        m_out = sem("m_left_out_expert_known")
        m_b2 = sem("m_bias_rows_ready")
        m_bzero = sem("m_raw_bias_rows_cleared")
        m_F = sem("m_hidden_in_psum")
        m_hi = sem("m_act_high_written")
        m_lo = sem("m_act_buffers_done_by_pool")
        m_O = sem("m_expert_out_in_psum")
        m_Oacc = sem("m_out_banks_free")
        m_x2 = sem("m_x2_tiles_written")
        a_raw = [sem(f"a_raw_{n}_loaded") for n in "qkv"]
        a_wps = sem("a_weights_transposed_in_psum")
        a_whi = sem("a_w_high_written")
        a_wlo = sem("a_w_low_written")
        a_const = sem("a_padding_and_ones_written")
        a_stage = sem("a_x_staged")
        a_T = sem("a_xT_in_psum")
        a_Thi = sem("a_xT_high_written")
        a_Tlo = sem("a_xT_low_written")
        a_proj = sem("a_projection_in_psum")
        a_part1 = sem("a_first_parts_written")
        a_rest = sem("a_rests_written")
        a_part2 = sem("a_second_parts_written")
        a_part3 = sem("a_third_parts_written")
        a_v = sem("a_v_copied")
        a_qT = sem("a_qT_written")
        a_kT = sem("a_kT_written")
        a_diag = sem("a_q_blocks_on_diagonal")
        a_vT = sem("a_vT_written")
        a_S = sem("a_scores_in_psum")
        a_shift = sem("a_scores_shifted")
        a_exp = sem("a_exps_ready")
        a_PT = sem("a_probs_transposed")
        a_PV = sem("a_context_in_psum")
        a_ctx = sem("a_context_normalised")
        a_x3 = sem("a_x3_tiles_written")
        p_rawu = sem("p_up_loaded")
        p_raws = sem("p_small_weights_loaded")
        p_rawd = sem("p_down_loaded")
        p_gb = sem("p_gamma_beta_loaded")
        p_whi = sem("p_w_high_written")
        p_wlo = sem("p_w_low_written")
        p_eTps = sem("p_expT_in_psum")
        p_eT = sem("p_expT_copied")
        p_ef = sem("p_expert_fc2_in_psum")
        p_efhi = sem("p_expert_fc2_high")
        p_eflo = sem("p_expert_fc2_low")
        p_g8 = sem("p_gate_split")
        p_stage = sem("p_x_staged")
        p_T = sem("p_xT_in_psum")
        p_Thi = sem("p_xT_high_written")
        p_Tlo = sem("p_xT_low_written")
        p_gps = sem("p_gate_rows_in_psum")
        p_rows = sem("p_gate_rows_copied")
        p_lps = sem("p_logits_in_psum")
        p_top = sem("p_logits_copied")
        p_U = sem("p_up_in_psum")
        p_relu = sem("p_relu_written")
        p_hi = sem("p_square_high_written")
        p_lo = sem("p_square_low_written")
        p_L = sem("p_latent_in_psum")
        p_Lhi = sem("p_latent_high_written")
        p_Llo = sem("p_latent_low_written")
        p_R = sem("p_routed_in_psum")
        p_Radd = sem("p_routed_added")
        p_D = sem("p_down_in_psum")
        p_Dadd = sem("p_down_banks_free")
        p_xb = sem("p_beta_added_to_residual")
        p_y = sem("p_output_tiles_ready")

        def bc(ap, shape):
            return ap.to_broadcast(shape) if not isinstance(ap, bass.AP) else ap.broadcast_to(shape)

        sc = small[:, 0:64].rearrange("p (l n m) -> p l n m", l=KB, n=B)
        mx = small[:, 64:80]
        stats = small[:, 80:86]
        mv = small[:, 86:118].rearrange("p (t c) -> p t c", c=2)
        rs = small[:, 118:134]
        nm = small[:, 134:150]
        hv = small[:, 150:166]
        magic = small[:, 166:168].bitcast(I32)

        absum = small2[:, 0:TB]
        statin = small2[:, 4:12].rearrange("p (t c) -> p t c", c=2)
        vmask = small2[:, 12:20].rearrange("p (t c) -> p t c", c=2)
        gbias = small2[:, 20:21]
        gw_last = small2[:, 21:22]
        gb_col = small2[:, 22:23]
        ratio = small2[:, 23:26]
        gwraw = small2[:, 26:38].rearrange("p (k e) -> p k e", e=E)
        b1c = small2[:, 38:50].rearrange("p (e f) -> p e f", f=KB)
        pr = small2[:, 50:62].rearrange("p (t e) -> p t e", e=E)
        coef = small2[:, 62:70].rearrange("p (s t) -> p s t", s=SL)
        is_low, sign = small2[0:2 * 32, 70:71], small2[0:2 * 32, 71:72]
        first = small2[:, 72:73]
        second = small2[:, 73:74]
        last3 = small2[:, 74:77]
        left_out = small2[:, 78:79].bitcast(I32)
        top = small2[:, 86:94].rearrange("p (i t) -> p i t", i=2)
        cmp3 = small2[:, 100:103]
        rank = small2[:, 103:106]
        tA, tB = small2[:, 106:110], small2[:, 110:114]
        stats4 = small2[:, 114:138].rearrange("p (t c) -> p t c", c=6)
        RELUS = len(relu)
        OB = 3
        mx3 = small2[:, 140:204].rearrange("p (u i) -> p u i", u=2)
        NP2 = NT // 2
        PROJ_BANK = (6, 7, 4, 5, 6, 7)
        G = P // 32
        g8raw = small2[:, 204:236].rearrange("p (k e) -> p k e", e=NE)
        logit8 = mx3.rearrange("p u i -> p (u i)")[:, 0:TB * NE].rearrange("p (t e) -> p t e", e=NE)
        top8 = mx3.rearrange("p u i -> p (u i)")[:, TB * NE:2 * TB * NE].rearrange("p (t e) -> p t e", e=NE)
        route = tA
        FUNCS = (ACT.Tanh, ACT.Gelu, ACT.Silu)

        block = ctx.enter_context(nc.Block())

        WB = [(j, e) for j in range(2) for e in range(E)]
        EARLY = 2 * E - 2
        VECTOR_MIXES = [(n, lb) for n in range(B - 1) for lb in range(KB)]
        POOL_MIXES = [(B - 1, lb) for lb in range(KB)]

        @block.sync
        def _(sp):
            sp.sem_inc(s_out, 1)
            for k in range(KB):
                cols = slice(k * P, (k + 1) * P)
                sp.dma_start(xs[:, :, cols], x.rearrange("b (t p) d -> p (b t) d", p=P)[:, :, cols]).then_inc(s_x[k], 16)

            def load_expert(q):
                j, e = WB[q]
                sp.dma_start(wraw[:, j, e, 1], (w1, w2)[j][e].rearrange("(k p) n -> p k n", p=P)
                             ).then_inc(s_raw[q], 16)

            with nc.allow_non_contiguous_dma("small columns"):
                sp.dma_start(gwraw, gate_w[0:D].rearrange("(k p) e -> p k e", p=P)).then_inc(m_consts, 16)
                sp.dma_start(gw_last[0:E], gate_w[D:D + 1].rearrange("o e -> e o")).then_inc(m_consts, 16)
                sp.dma_start(gb_col[0:E], gate_b.rearrange("(e o) -> e o", o=1)).then_inc(m_consts, 16)
                sp.dma_start(b1c, b1.rearrange("e (f p) -> p e f", p=P)).then_inc(m_consts, 16)
                sp.wait_ge(m_bzero, 1)
                for half in range(2):
                    sp.dma_start(bias_raw[half * E:half * E + E], b2).then_inc(m_consts, 16)
                    for j, b in enumerate((bq, bk, bv)):
                        row = 32 + half * E + j
                        sp.dma_start(bias_raw[row:row + 1], b.rearrange("(o d) -> o d", o=1)).then_inc(m_consts, 16)
            for q in range(EARLY):
                load_expert(q)
            sp.wait_ge(s_y, len(VECTOR_MIXES))
            sp.wait_ge(s_y_pool, len(POOL_MIXES))
            for q in range(EARLY, 2 * E):
                load_expert(q)
            with sp.Fori(0, B - 1) as c:
                sp.wait_ge(m_abs, c + 1)
                sp.sem_inc(s_settled, 1)
                sp.wait_ge(s_x1, TB * c + 2 * TB)
                sp.sem_inc(s_settled, 1)
                sp.dma_start(stage[:], xs[:, bass.ds(TB * c + TB, TB)]).then_inc(m_stage, 16)
            sp.wait_ge(m_F, SL * KB * B)
            sp.dma_start(rawq[:, 0], wq.rearrange("(o p) i -> p o i", p=P)).then_inc(a_raw[0], 16)
            sp.dma_start(rawq[:, 1], wk.rearrange("(o p) i -> p o i", p=P)).then_inc(a_raw[1], 16)
            sp.dma_start(rawq[:, 2], wv.rearrange("(o p) i -> p o i", p=P)).then_inc(a_raw[2], 16)
            sp.wait_ge(m_abs, B)
            sp.dma_start(stage3[:], xs[:, 0:2]).then_inc(a_stage, 16)
            sp.wait_ge(a_T, 2)
            sp.dma_start(stage3[:], xs[:, 2:4]).then_inc(a_stage, 16)
            sp.wait_ge(a_wps, 3 * KB)
            sp.dma_start(rawu[:], up_w.rearrange("(k p) n -> p k n", p=P)).then_inc(p_rawu, 16)
            sp.dma_start(raw1[:], fc1_w.rearrange("(k p) n -> p k n", p=P)).then_inc(p_raws, 16)
            sp.dma_start(raw2[:], fc2_w.rearrange("(k p) n -> p k n", p=P)).then_inc(p_raws, 16)
            sp.dma_start(rawe[:], expert_w.rearrange("(k p) n -> p k n", p=P)).then_inc(p_raws, 16)
            sp.dma_start(g8raw, gate8_w.rearrange("(k p) n -> p k n", p=P)).then_inc(p_raws, 16)
            sp.wait_ge(m_x2, NT)
            with sp.Fori(0, NP2 - 2) as p:
                sp.wait_ge(a_T, 2 * p + 4)
                sp.sem_inc(s_settled, 1)
                sp.dma_start(stage3[:], xs[:, bass.ds(2 * p + 4, 2)]).then_inc(a_stage, 16)
            sp.wait_ge(a_proj, 6 * NP2)
            sp.dma_start(rawd[:], down_w.rearrange("(k p) n -> p k n", p=P)).then_inc(p_rawd, 16)
            sp.wait_ge(a_T, 2 * NP2)
            sp.wait_ge(a_diag, 16 * NP2 - 8)
            sp.wait_ge(a_x3, TB)
            sp.dma_start(stage4[:], xs[:, 0:TB]).then_inc(p_stage, 16)
            sp.wait_ge(p_wlo, KB + 1 + TB)
            sp.dma_start(gam_b[:], gamma.partition_broadcast(P)).then_inc(p_gb, 16)
            sp.dma_start(bet_b[:], beta.partition_broadcast(P)).then_inc(p_gb, 16)
            sp.wait_ge(a_x3, NT)
            out_tiles = out.rearrange("b (t p) d -> (b t) p d", p=P)

            def store(c):
                for t in range(TB):
                    sp.wait_ge(p_y, TB * c + (t + 1))
                    sp.sem_inc(s_settled, 1)
                    sp.dma_start(out_tiles[TB * c + t], acc4[:, t]).then_inc(s_out, 16)

            with sp.Fori(0, B - 1) as c:
                sp.wait_ge(p_T, KB * c + KB)
                sp.sem_inc(s_settled, 1)
                sp.dma_start(stage4[:], xs[:, bass.ds(TB * c + TB, TB)]).then_inc(p_stage, 16)
                store(c)
            store(B - 1)
            sp.wait_ge(s_out, 16 * NT + 1)

        @block.gpsimd
        def _(pool):
            ch = Chain(pool, s_gch)
            ch.link(pool.memset(ident[:], 0.0))
            pool.affine_select(out=ident[:], in_=ident[:], compare_op=ALU.not_equal, fill=1.0,
                               base=0, pattern=[[-1, P]], channel_multiplier=1).then_inc(s_ident, 1)
            pool.memset(bias_raw[:], 0.0).then_inc(m_bzero, 1)
            ch.link(pool.memset(ones[:], 1.0))
            ch.link(pool.memset(gwp[:].bitcast(F32), 0.0))
            ch.link(pool.memset(vmask, 0.0))
            for t in range(TB):
                lo = VIS - t * P
                if lo >= P:
                    ch.link(pool.memset(vmask[:, t, 1:2], 1.0 / (VIS * D)))
                elif lo <= 0:
                    ch.link(pool.memset(vmask[:, t, 0:1], 1.0 / ((S - VIS) * D)))
                else:
                    ch.link(pool.memset(vmask[:, t, 1:2], 1.0 / (VIS * D)))
                    ch.link(pool.memset(vmask[:, t, 0:1], 1.0 / ((S - VIS) * D)))
                    ch.link(pool.affine_select(out=vmask[:, t, 1:2], in_=vmask[:, t, 1:2], compare_op=ALU.is_ge,
                                               fill=0.0, base=lo - 1, pattern=[[0, 1]], channel_multiplier=-1))
                    ch.link(pool.affine_select(out=vmask[:, t, 0:1], in_=vmask[:, t, 0:1], compare_op=ALU.is_ge,
                                               fill=0.0, base=-lo, pattern=[[0, 1]], channel_multiplier=1))
            pool.wait_ge(m_consts, 16 * 12)
            ch.link(pool.tensor_copy(gwp[:, 0, :, 0:E], gwraw))
            pool.tensor_tensor(gwp[:, 1, :, 0:E], gwraw, gwp[:, 0, :, 0:E].bitcast(F32),
                               ALU.subtract).then_inc(m_gwp, 1)

            def w_low(q):
                j, e = WB[q]
                pool.wait_ge(s_whi, q + 1)
                pool.tensor_tensor(wf[:, j, e, 1], wraw[:, j, e, 1], wf[:, j, e, 0].bitcast(F32),
                                   ALU.subtract).then_inc(s_wlo, 1)

            w_low(0)
            w_low(1)
            for n, lb in POOL_MIXES:
                for m in range(1, B):
                    i = (B - 1) * lb + m - 1
                    pool.wait_ge(s_terms, B * lb + m + 1)
                    ins = pool.tensor_tensor(yT[:, n, lb, :], yT[:, n, lb, :], terms[:, i % 8], ALU.add)
                    if m < B - 1:
                        ch.link(ins)
                    else:
                        ins.then_inc(s_y_pool, 1)
            for q in range(2, 2 * E):
                w_low(q)

            def low_halves(c):
                for j in range(SL * KB):
                    slot, f = j // KB, j % KB
                    pool.wait_ge(m_hi, SL * KB * c + (j + 1))
                    pool.tensor_tensor(a2[:, slot, 1, f], act32[:, j % 2], a2[:, slot, 0, f].bitcast(F32),
                                       ALU.subtract).then_inc(m_lo, 1)

            pool.sem_inc(m_lo, 2)
            with pool.Fori(0, B) as c:
                low_halves(c)

            pool.wait_ge(m_O, SL * TB * B)
            pool.memset(qdiag[:], 0.0).then_inc(a_const, 1)
            pool.memset(vT[:, :, DH, :], 1.0).then_inc(a_const, 1)

            def by_pairs(t, u):
                return t[:, u].rearrange("p (i j d) -> p i j d", j=2, d=DH)

            def part(t, u, n):
                return t[:, u, n].rearrange("p i d j -> p i j d")

            with pool.Fori(0, NP2) as p:
                for i in range(4):
                    u, dst = i // 2, (q3, k3)[i % 2]
                    pool.wait_ge(a_part2, 4 * p + (i + 1))
                    pool.tensor_tensor(part(dst, u, 2), by_pairs(rest, i % 2), part(dst, u, 1),
                                       ALU.subtract).then_inc(a_part3, 1)

            pool.wait_ge(p_raws, 64)
            pool.wait_ge(a_kT, 6 * NP2)
            ch.link(pool.memset(g8p[:].bitcast(F32), 0.0))
            ch.link(pool.tensor_copy(g8p[:, 0, :, 0:NE], g8raw))
            pool.tensor_tensor(g8p[:, 1, :, 0:NE], g8raw, g8p[:, 0, :, 0:NE].bitcast(F32),
                               ALU.subtract).then_inc(p_g8, 1)
            for k in range(KB):
                pool.wait_ge(p_whi, k + 1)
                pool.tensor_tensor(wup[:, 1, k], rawu[:, k], wup[:, 0, k].bitcast(F32), ALU.subtract).then_inc(p_wlo, 1)
            pool.wait_ge(p_whi, KB + 1)
            pool.tensor_tensor(wf1[:, 1], raw1[:], wf1[:, 0].bitcast(F32), ALU.subtract).then_inc(p_wlo, 1)
            for k in range(0, NU, 2):
                if k == 0:
                    pool.wait_ge(p_wlo, 1 + KB)
                    pool.wait_ge(p_ef, NL)
                if k == NU // 2:
                    pool.wait_ge(a_PV, NP2)
                pool.wait_ge(p_whi, KB + 2 + k // 2)
                pool.tensor_tensor(wdn[:, 1, k:k + 2], rawd[:, k:k + 2], wdn[:, 0, k:k + 2].bitcast(F32),
                                   ALU.subtract).then_inc(p_wlo, 1)

            def p_square_low(c, i):
                pool.wait_ge(p_relu, NU * c + (i + 1))
                pool.wait_ge(p_lo, NU * c + (i + RELUS))
                ch.link(pool.tensor_tensor(sq32[:], relu[i % RELUS][:], relu[i % RELUS][:], ALU.mult))
                pool.wait_ge(p_hi, NU * c + (i + 1))
                pool.tensor_tensor(hh[:, i, 1], sq32[:], hh[:, i, 0].bitcast(F32), ALU.subtract).then_inc(p_lo, 1)

            pool.sem_inc(p_lo, RELUS)
            pool.wait_ge(p_gb, 32)
            ch.end()
            with pool.Fori(0, B) as c:
                ch.begin(c, NU)
                for i in range(NU):
                    p_square_low(c, i)
                pool.wait_ge(p_stage, 16 * c + 16)
                for t in range(TB):
                    pool.tensor_tensor(xs[:, TB * c + t], xs[:, TB * c + t], bet_b[:], ALU.add).then_inc(p_xb, 1)
            ch.end(B)

        @block.tensor
        def _(pe):
            pe.wait_ge(s_ident, 1)
            for lb in range(KB):
                pe.wait_ge(s_x[lb], 16)
                for n in range(B):
                    job = B * lb + n
                    if job >= 8:
                        pe.wait_ge(s_xt, job - 7)
                    for t in range(TB):
                        mm = pe.transpose(ps[:, job % 8, t * P:(t + 1) * P],
                                          xs[:, TB * n + t, lb * P:(lb + 1) * P], ident[:])
                    mm.then_inc(s_xt_ps, 1)

            def mixed_back(n):
                for lb in range(KB):
                    job = KB * n + lb
                    if (n, lb) in VECTOR_MIXES:
                        pe.wait_ge(s_y, VECTOR_MIXES.index((n, lb)) + 1)
                    else:
                        pe.wait_ge(s_y_pool, POOL_MIXES.index((n, lb)) + 1)
                    if job >= OB:
                        pe.wait_ge(s_ycp, job - (OB - 1))
                    else:
                        pe.wait_ge(s_xt, B * KB)
                    for t in range(TB):
                        mm = pe.transpose(ps[:, 4 + job % OB, t * P:(t + 1) * P],
                                          yT[:, n, lb, t * P:(t + 1) * P], ident[:])
                    mm.then_inc(s_yt, 1)

            mixed_back(0)
            def split3(dst, w_hi, w_lo, x_hi, x_lo, first, last):
                pe.matmul(dst, w_hi, x_hi, start=first, stop=False)
                pe.matmul(dst, w_hi, x_lo, start=False, stop=False)
                return pe.matmul(dst, w_lo, x_hi, start=False, stop=last)

            def m_transposes(c, first=False):
                if first:
                    pe.wait_ge(s_x1, TB)
                else:
                    pe.wait_ge(m_stage, 16 * c)
                for k in range(KB):
                    if not first:
                        pe.wait_ge(m_hi, SL * KB * c - (KB - k - 1))
                    for t in range(TB):
                        mm = pe.transpose(ps[:, k, t * P:(t + 1) * P],
                                          (xs if first else stage)[:, t, k * P:(k + 1) * P], ident[:])
                    mm.then_inc(m_T, 1)

            def m_stats(c):
                pe.wait_ge(m_stat, c + 1)
                for t in range(TB):
                    mm = pe.matmul(ps[:, 7, 0:2], ones[:], statin[:, t], start=(t == 0), stop=(t == TB - 1))
                mm.then_inc(m_statps, 1)

            def m_gate(c):
                pe.wait_ge(m_Thi, KB * c + KB)
                pe.wait_ge(m_Tlo, KB * c + KB)
                pe.wait_ge(m_gbias, c + 1)
                for k in range(KB):
                    mm = split3(ps[:, 7, :], gwp[:, 0, k], gwp[:, 1, k], xth[:, 0, k], xth[:, 1, k],
                                k == 0, k == KB - 1)
                mm.then_inc(m_gps, 1)

            def m_logits(c):
                pe.wait_ge(m_rows, c + 1)
                for t in range(TB):
                    mm = pe.matmul(ps[:, 7, 4 * t:4 * t + E], rowsE[:, t * P:(t + 1) * P], ident[0:E, 0:E],
                                   start=True, stop=True)
                mm.then_inc(m_lps, 1)

            def m_first_token(c):
                pe.wait_ge(m_prob, c + 1)
                pe.matmul(ps[:, 7, 0:E], ones[0:1, :], pr[0:1, 0, :], start=True, stop=True).then_inc(m_t0, 1)

            def m_hidden(c, slot, e):
                for f in range(KB):
                    if slot == 0 and f == 0:
                        pe.wait_ge(m_Thi, KB * c + KB)
                        pe.wait_ge(m_Tlo, KB * c + KB)
                    if slot == 1:
                        pe.wait_ge(m_hi, SL * KB * c + (f + 1))
                    for k in range(KB):
                        mm = split3(ps[:, f], wf[:, 0, e, 0, k, f * P:(f + 1) * P],
                                    wf[:, 0, e, 1, k, f * P:(f + 1) * P], xth[:, 0, k], xth[:, 1, k],
                                    k == 0, k == KB - 1)
                    mm.then_inc(m_F, 1)

            def m_outp(c, slot, e, tiles):
                for t in tiles:
                    j = slot * TB + t
                    if t == 0:
                        pe.wait_ge(m_hi, SL * KB * c + KB * (slot + 1))
                        pe.wait_ge(m_lo, SL * KB * c + (KB * (slot + 1) + 2))
                    pe.wait_ge(m_Oacc, SL * TB * c + (max(j, OB - 1) + 1))
                    b = 4 + j % OB
                    pe.matmul(ps[:, b], pick[0:2 * E, e], bias_rows[0:2 * E], start=True, stop=False)
                    for k in range(KB):
                        mm = split3(ps[:, b], a2[:, slot, 0, k, t * P:(t + 1) * P], a2[:, slot, 1, k, t * P:(t + 1) * P],
                                    wf[:, 1, e, 0, k], wf[:, 1, e, 1, k], False, k == KB - 1)
                    mm.then_inc(m_O, 1)

            def m_slot(unused, slot, part):
                if slot == 0:
                    with pe.If(unused == 0):
                        part(1)
                    with pe.Else():
                        part(0)
                else:
                    with pe.If(unused == 2):
                        part(1)
                    with pe.Else():
                        part(2)

            def m_chunk(c, more):
                pe.wait_ge(m_out, c + 1)
                pe.sem_inc(s_settled, 1)
                unused = pe.value_load(left_out[0:1, 0:1], min_val=0, max_val=E - 1)
                m_slot(unused, 0, lambda e: m_hidden(c, 0, e))
                m_slot(unused, 1, lambda e: m_hidden(c, 1, e))
                pe.wait_ge(m_b2, 1)
                pe.wait_ge(s_whi, 2 * E)
                pe.wait_ge(s_wlo, 2 * E)
                m_slot(unused, 0, lambda e: m_outp(c, 0, e, (0, 1)))
                if more:
                    m_transposes(c + 1)
                m_slot(unused, 0, lambda e: m_outp(c, 0, e, (2, 3)))
                if more:
                    m_stats(c + 1)
                else:
                    a_weights(0)
                m_slot(unused, 1, lambda e: m_outp(c, 1, e, (0,)))
                if more:
                    m_gate(c + 1)
                else:
                    a_weights(1)
                m_slot(unused, 1, lambda e: m_outp(c, 1, e, (1,)))
                if more:
                    m_logits(c + 1)
                m_slot(unused, 1, lambda e: m_outp(c, 1, e, (2,)))
                if more:
                    m_first_token(c + 1)
                m_slot(unused, 1, lambda e: m_outp(c, 1, e, (3,)))
                if not more:
                    a_weights(2)

            def a_weights(j):
                pe.wait_ge(a_raw[j], 16)
                for k in range(KB):
                    if j == 0:
                        pe.wait_ge(m_hi, SL * KB * B - (KB - 1 - k))
                    else:
                        pe.wait_ge(a_wlo, KB * (j - 1) + k + 1)
                    for o in range(KB):
                        mm = pe.transpose(ps[:, k, o * P:(o + 1) * P], rawq[:, j, o, k * P:(k + 1) * P], ident[:])
                    mm.then_inc(a_wps, 1)

            m_transposes(0, first=True)
            pe.wait_ge(m_gwp, 1)
            m_stats(0)
            m_gate(0)
            m_logits(0)
            mixed_back(1)
            mixed_back(2)
            m_first_token(0)
            mixed_back(3)
            pe.wait_ge(s_ycp, B * KB)
            pe.wait_ge(s_whi, E)
            pe.wait_ge(s_wlo, E)
            with pe.Fori(0, B - 1) as c:
                m_chunk(c, True)
            m_chunk(B - 1, False)

            def a_transposes(p, first=False):
                pe.wait_ge(a_stage, 16 * p + 16)
                for k in range(KB):
                    if first and k == 0:
                        pe.wait_ge(m_Oacc, SL * TB * B + OB)
                    elif not first and k == 0:
                        pe.wait_ge(a_v, 2 * p - 1)
                    elif not first and k == 2:
                        pe.wait_ge(a_rest, 4 * p - 1)
                    for u in range(2):
                        mm = pe.transpose(ps[:, 4 + k // 2, ((k % 2) * 2 + u) * P:((k % 2) * 2 + u + 1) * P],
                                          stage3[:, u, k * P:(k + 1) * P], ident[:])
                    if k % 2:
                        mm.then_inc(a_T, 1)

            def a_project(p, job, first=False):
                u, j = job // 3, job % 3
                if job == 0:
                    pe.wait_ge(a_Thi, 2 * p + 2)
                    pe.wait_ge(a_Tlo, 2 * p + 2)
                    if not first:
                        pe.wait_ge(a_rest, 4 * p)
                elif job == 1 and not first:
                    pe.wait_ge(a_v, 2 * p)
                elif job >= 4:
                    pe.wait_ge(a_rest, 4 * p + (job - 3))
                if first and u == 0:
                    pe.wait_ge(a_whi, KB * (j + 1))
                    pe.wait_ge(a_wlo, KB * (j + 1))
                bank = ps[:, PROJ_BANK[job]]
                for k in range(KB):
                    split3(bank, xt3[:, 0, k, u * P:(u + 1) * P], xt3[:, 1, k, u * P:(u + 1) * P],
                           wqkv[:, j, 0, k], wqkv[:, j, 1, k], k == 0, False)
                pe.matmul(bank, pick[32:32 + 2 * E, j], bias_rows[32:32 + 2 * E],
                          start=False, stop=True).then_inc(a_proj, 1)

            def a_scores(p, u):
                pe.wait_ge(a_diag, 16 * p + (8 * u + 8))
                pe.wait_ge(a_kT, 6 * p + (3 * u + 3))
                pe.wait_ge(a_ctx, 2 * p + (u + 1))
                for tok in range(32):
                    dst = ps[:, 2 * u + tok // 16, (tok % 16) * H:(tok % 16 + 1) * H]
                    for i, (vq, vk) in enumerate(((0, 0), (0, 1), (1, 2))):
                        mm = pe.matmul(dst, qdiag[:, vq, tok], kT[:, u, vk, tok], start=(i == 0), stop=(i == 2))
                mm.then_inc(a_S, 1)

            def a_context(p):
                pe.wait_ge(a_PT, 2 * p + 2)
                pe.wait_ge(a_vT, 2 * p + 2)
                pe.sem_inc(s_settled, 1)
                for step in range(4):
                    for i in range(16):
                        for g in range(G):
                            bank = (g + step) % 4
                            u, tok, rows = bank // 2, (bank % 2) * 16 + i, slice(32 * g, 32 * g + 32)
                            mm = pe.matmul(ps[rows, bank, i * (DH + 1):(i + 1) * (DH + 1)],
                                           pT[rows, u, tok, :], vT[rows, u, :, tok], start=True, stop=True)
                mm.then_inc(a_PV, 1)

            a_transposes(0, first=True)
            for job in range(6):
                a_project(0, job, first=True)
            a_transposes(1)

            def a_pair(p, more_T):
                a_project(p + 1, 0)
                a_scores(p, 0)
                a_project(p + 1, 1)
                a_project(p + 1, 2)
                a_scores(p, 1)
                for job in (3, 4, 5):
                    a_project(p + 1, job)
                if more_T:
                    a_transposes(p + 2)
                a_context(p)

            with pe.Fori(0, NP2 - 2) as p:
                a_pair(p, True)
            a_pair(NP2 - 2, False)

            def p_transposes(c, banks, blocks=range(KB)):
                pe.wait_ge(p_stage, 16 * c + 16)
                for k in blocks:
                    if banks is FIRST_BANKS and k >= 2:
                        pe.wait_ge(p_Tlo, k - 1)
                    if banks is LOOP_BANKS:
                        if k < 2:
                            pe.wait_ge(p_relu, NU * c - (1 - k))
                        else:
                            pe.wait_ge(p_Llo, NL * c - (3 - k))
                    for t in range(TB):
                        mm = pe.transpose(ps[:, banks[k], t * P:(t + 1) * P], stage4[:, t, k * P:(k + 1) * P], ident[:])
                    mm.then_inc(p_T, 1)

            def p_gate(c):
                pe.wait_ge(p_Thi, KB * c + KB)
                pe.wait_ge(p_Tlo, KB * c + KB)
                pe.wait_ge(p_top, c)
                for k in range(KB):
                    mm = split3(ps[:, 7, :], g8p[:, 0, k], g8p[:, 1, k], xth[:, 0, k], xth[:, 1, k],
                                k == 0, k == KB - 1)
                mm.then_inc(p_gps, 1)

            def p_up(c, i):
                if i == 0:
                    pe.wait_ge(p_Tlo, KB * c + KB)
                if i >= 4:
                    pe.wait_ge(p_relu, NU * c + (i - 3))
                for k in range(KB):
                    mm = split3(ps[:, i % 4, :], wup[:, 0, k, i * P:(i + 1) * P], wup[:, 1, k, i * P:(i + 1) * P],
                                xth[:, 0, k], xth[:, 1, k], k == 0, k == KB - 1)
                mm.then_inc(p_U, 1)

            def p_latent(c, b):
                pe.wait_ge(p_relu, NU * c + (5 + b))
                for k in range(KB):
                    mm = split3(ps[:, b, :], wf1[:, 0, k, b * P:(b + 1) * P], wf1[:, 1, k, b * P:(b + 1) * P],
                                xth[:, 0, k], xth[:, 1, k], k == 0, k == KB - 1)
                mm.then_inc(p_L, 1)

            def p_down(c, t):
                tok = slice(t * P, (t + 1) * P)
                if t == 0:
                    pe.wait_ge(p_Lhi, NL * c + NL)
                    pe.wait_ge(p_Llo, NL * c + NL)
                pe.wait_ge(p_Radd, TB * c + (t + 1))
                for k in range(NL):
                    mm = split3(ps[:, 6, :], lat[:, 0, k, tok], lat[:, 1, k, tok], wef[:, 0, k], wef[:, 1, k],
                                k == 0, k == NL - 1)
                mm.then_inc(p_R, 1)
                if t == 0:
                    pe.wait_ge(p_hi, NU * c + NU)
                    pe.wait_ge(p_lo, NU * c + (NU + RELUS))
                    pe.wait_ge(p_wlo, 1 + KB + NU // 2)
                pe.wait_ge(p_Dadd, TB * c + (t + 1))
                for k in range(NU):
                    mm = split3(ps[:, 4 + t % 2, :], hh[:, k, 0, tok], hh[:, k, 1, tok], wdn[:, 0, k], wdn[:, 1, k],
                                k == 0, k == NU - 1)
                mm.then_inc(p_D, 1)

            def p_chunk(c, more):
                for i in range(4):
                    p_up(c, i)
                pe.wait_ge(p_rows, c + 1)
                pe.sem_inc(s_settled, 1)
                for t in range(TB):
                    mm = pe.matmul(ps[:, 7, NE * t:NE * t + NE], rows8[:, t * P:(t + 1) * P], ident[0:NE, 0:NE],
                                   start=True, stop=True)
                mm.then_inc(p_lps, 1)
                for i in range(4, NU):
                    p_up(c, i)
                for b in range(NL):
                    p_latent(c, b)
                if more:
                    p_transposes(c + 1, LOOP_BANKS)
                p_down(c, 0)
                p_down(c, 1)
                if more:
                    p_gate(c + 1)
                p_down(c, 2)
                p_down(c, 3)

            LOOP_BANKS, FIRST_BANKS = (2, 3, 0, 1), (4, 5, 4, 5)
            pe.wait_ge(p_raws, 64)
            pe.wait_ge(a_rest, 4 * NP2)
            for m in range(NL):
                for l in range(NL):
                    mm = pe.transpose(ps[:, 6, m * LAT + l * P:m * LAT + (l + 1) * P],
                                      rawe[:, l, m * P:(m + 1) * P], ident[:])
            mm.then_inc(p_eTps, 1)
            a_scores(NP2 - 1, 0)
            pe.wait_ge(p_eT, 1)
            for l in range(NL):
                for m in range(NL):
                    mm = pe.matmul(ps[:, 7 - l, :], expT[:, m, l * P:(l + 1) * P], raw2[:, m],
                                   start=(m == 0), stop=(m == NL - 1))
                mm.then_inc(p_ef, 1)
            p_transposes(0, FIRST_BANKS, (0, 1))
            a_scores(NP2 - 1, 1)
            p_transposes(0, FIRST_BANKS, (2, 3))
            a_context(NP2 - 1)
            pe.wait_ge(p_g8, 1)
            pe.wait_ge(p_eflo, NL)
            p_gate(0)
            pe.wait_ge(p_wlo, 1 + KB)
            pe.wait_ge(a_ctx, 2 * NP2 + 2)
            with pe.Fori(0, B - 1) as c:
                p_chunk(c, True)
            p_chunk(B - 1, False)

        @block.scalar
        def _(act):
            ch = Chain(act, s_ach)
            for lb in range(KB):
                for n in range(B):
                    job = B * lb + n
                    act.wait_ge(s_xt_ps, job + 1)
                    act.copy(xT[:, lb, n, :], ps[:, job % 8, :]).then_inc(s_xt, 1)
                for n in range(B):
                    act.wait_ge(s_xt, B * lb + n + 1)
                    if lb or n:
                        act.wait_ge(s_sq, B * lb + n)
                    act.activation(dump[:, 1], xT[:, lb, n, :], ACT.Square,
                                   accum_out=sc[:, lb, n, n:n + 1]).then_inc(s_sq, 1)

            def w_high(q):
                j, e = WB[q]
                act.wait_ge(s_raw[q], 16)
                act.copy(wf[:, j, e, 0], wraw[:, j, e, 1]).then_inc(s_whi, 1)

            def first_terms(n):
                for lb in range(KB):
                    act.activation(yT[:, n, lb, :], xT[:, lb, 0, :], ACT.Copy,
                                   scale=sc[:, lb, n, 0:1]).then_inc(s_y0, 1)

            def copy_back(n):
                for lb in range(KB):
                    job = KB * n + lb
                    act.wait_ge(s_yt, job + 1)
                    act.copy(xs[:, TB * n:TB * n + TB, lb * P:(lb + 1) * P],
                             ps[:, 4 + job % OB, :].rearrange("p (t c) -> p t c", c=P)).then_inc(s_ycp, 1)

            def terms_for_pool(lb):
                n = B - 1
                for m in range(B):
                    i = (B - 1) * lb + m - 1
                    if m and i >= 8:
                        act.wait_ge(s_y_pool, (i - 8) // (B - 1) + 1)
                    act.activation(terms[:, i % 8] if m else yT[:, n, lb, :], xT[:, lb, m, :], ACT.Copy,
                                   scale=sc[:, lb, n, m:m + 1]).then_inc(s_terms, 1)

            w_high(0)
            w_high(1)
            act.wait_ge(s_pexp_in, 1)
            act.activation(sc[:, :, :, :], sc[:, :, :, :], ACT.Exp, scale=float(D) ** -0.5).then_inc(s_pexp, 1)
            act.wait_ge(s_mixw, 1)
            first_terms(0)
            first_terms(1)
            terms_for_pool(0)
            terms_for_pool(1)
            copy_back(0)
            first_terms(2)
            terms_for_pool(2)
            w_high(2)
            terms_for_pool(3)

            def m_prep(c, last_F=None):
                for k in range(KB):
                    act.wait_ge(m_T, KB * c + (k + 1))
                    if k == 0 and last_F is not None:
                        act.wait_ge(m_F, last_F)
                    act.copy(xth[:, 0, k], ps[:, k, :]).then_inc(m_Thi, 1)
                for t in range(TB):
                    src, dst = (xs[:, t], dump[:, t % 2]) if last_F is None else (stage[:, t], stage[:, t])
                    ins = act.activation(dst, src, ACT.Abs, accum_out=absum[:, t:t + 1])
                    if t < TB - 1:
                        ch.link(ins)
                    else:
                        ins.then_inc(m_abs, 1)

            def m_rowcopy(c):
                act.wait_ge(m_gps, c + 1)
                act.wait_ge(m_gbias, c + 1)
                act.activation(rowsE[:], ps[0:E, 7, :], ACT.Identity, bias=gbias[0:E]).then_inc(m_rows, 1)

            def m_softmax(c):
                act.wait_ge(m_shift, c + 1)
                act.activation(pr, pr, ACT.Exp).then_inc(m_exp, 1)

            def m_acts(c, slot, e):
                for f in range(KB):
                    j = slot * KB + f
                    act.wait_ge(m_F, SL * KB * c + (j + 1))
                    act.wait_ge(m_lo, SL * KB * c + (j + 1))
                    act.activation(act32[:, j % 2], ps[:, f, :], FUNCS[e], bias=b1c[:, e, f:f + 1])
                    act.activation(a2[:, slot, 0, f], ps[:, f, :], FUNCS[e], bias=b1c[:, e, f:f + 1]).then_inc(m_hi, 1)

            def m_chunk(c, more):
                act.wait_ge(m_out, c + 1)
                act.sem_inc(s_settled, 1)
                unused = act.value_load(left_out[0:1, 0:1], min_val=0, max_val=E - 1)
                with act.If(unused == 0):
                    m_acts(c, 0, 1)
                with act.Else():
                    m_acts(c, 0, 0)
                with act.If(unused == 2):
                    m_acts(c, 1, 1)
                with act.Else():
                    m_acts(c, 1, 2)
                if more:
                    m_prep(c + 1, SL * KB * c + SL * KB)
                    m_rowcopy(c + 1)
                    m_softmax(c + 1)
                else:
                    for jk in range(3 * KB):
                        j, k = jk // KB, jk % KB
                        act.wait_ge(a_wps, jk + 1)
                        if jk == 0:
                            act.wait_ge(m_F, SL * KB * B)
                        elif jk == KB:
                            act.wait_ge(m_O, SL * TB * C3 + TB)
                        elif jk == 2 * KB:
                            act.wait_ge(m_O, SL * TB * B)
                        act.copy(wqkv[:, j, 0, k], ps[:, k, :]).then_inc(a_whi, 1)

            m_prep(0)
            w_high(3)
            act.wait_ge(m_gwp, 1)
            m_rowcopy(0)
            copy_back(1)
            m_softmax(0)
            copy_back(2)
            copy_back(3)
            w_high(4)
            w_high(5)
            C3 = B - 1
            with act.Fori(0, B - 1) as c:
                m_chunk(c, True)
            m_chunk(B - 1, False)

            def a_highs(p):
                for h in range(2):
                    act.wait_ge(a_T, 2 * p + (h + 1))
                    if h == 0:
                        act.wait_ge(a_proj, 6 * p)
                    act.copy(xt3[:, 0, 2 * h:2 * h + 2], ps[:, 4 + h, :].rearrange("p (k t) -> p k t", k=2)
                             ).then_inc(a_Thi, 1)

            def a_exp_shifted(p, u):
                act.wait_ge(a_shift, 2 * p + (u + 1))
                act.activation(sh[:, u], sh[:, u], ACT.Exp, scale=DH ** -0.5).then_inc(a_exp, 1)

            def by_pairs(t):
                return t.rearrange("p (i j d) -> p i j d", j=2, d=DH)

            def part(t, u, n):
                return t[:, u, n].rearrange("p i d j -> p i j d")

            def a_first_part(p, job, first=False):
                u, j = job // 3, job % 3
                act.wait_ge(a_proj, 6 * p + (job + 1))
                if not first:
                    act.wait_ge(*((a_qT, 4 * p + (2 * u - 2)), (a_kT, 6 * p + (3 * u - 3)))[j])
                act.copy(part((q3, k3)[j], u, 0), by_pairs(ps[:, PROJ_BANK[job], :])).then_inc(a_part1, 1)

            def a_copy_v(p, u, first=False):
                act.wait_ge(a_proj, 6 * p + (3 * u + 3))
                if not first:
                    act.wait_ge(a_vT, 2 * p)
                act.copy(vs[:, u], ps[:, PROJ_BANK[3 * u + 2], :]).then_inc(a_v, 1)

            def a_diagonal(p, u, first=False, groups=range(G)):
                act.wait_ge(a_qT, 4 * p + (2 * u + 2))
                if not first:
                    act.wait_ge(a_S, 2 * p + u)
                for g in groups:
                    rows = slice(32 * g, 32 * g + 32)
                    act.copy(qdiag[rows, 0, :, rows], qT[u][rows, 0]).then_inc(a_diag, 1)

            def a_pair(p, more_T):
                a_first_part(p + 1, 0)
                a_diagonal(p, 1)
                a_first_part(p + 1, 1)
                a_exp_shifted(p, 0)
                a_copy_v(p + 1, 0)
                a_diagonal(p + 1, 0)
                a_first_part(p + 1, 3)
                a_exp_shifted(p, 1)
                a_first_part(p + 1, 4)
                a_copy_v(p + 1, 1)
                if more_T:
                    a_highs(p + 2)

            a_highs(0)
            a_first_part(0, 0, first=True)
            a_first_part(0, 1, first=True)
            act.wait_ge(a_const, 2)
            a_diagonal(0, 0, first=True)
            a_copy_v(0, 0, first=True)
            a_first_part(0, 3, first=True)
            a_first_part(0, 4, first=True)
            a_copy_v(0, 1, first=True)
            a_highs(1)
            with act.Fori(0, NP2 - 2) as p:
                a_pair(p, True)
            a_pair(NP2 - 2, False)

            act.wait_ge(p_eTps, 1)
            act.copy(expT[:], ps[:, 6, :].rearrange("p (m l) -> p m l", m=NL)).then_inc(p_eT, 1)
            a_diagonal(NP2 - 1, 1, groups=(0, 1))
            a_exp_shifted(NP2 - 1, 0)

            def p_highs(c, banks, blocks=range(KB)):
                for k in blocks:
                    act.wait_ge(p_T, KB * c + (k + 1))
                    if k == 0 and banks is LOOP_BANKS:
                        act.wait_ge(p_L, NL * c)
                    act.copy(xth[:, 0, k], ps[:, banks[k], :]).then_inc(p_Thi, 1)

            def p_rowcopy(c):
                act.wait_ge(p_gps, c + 1)
                act.copy(rows8[:], ps[0:NE, 7, :]).then_inc(p_rows, 1)

            def p_square(c, i):
                act.wait_ge(p_U, NU * c + (i + 1))
                act.wait_ge(p_lo, NU * c + (i + 1))
                act.activation(relu[i % RELUS][:], ps[:, i % 4, :], ACT.Relu).then_inc(p_relu, 1)
                act.wait_ge(p_relu, NU * c + (i + 1))
                if i == NU // 2:
                    act.wait_ge(a_x3, NT)
                act.activation(hh[:, i, 0], relu[i % RELUS][:], ACT.Square).then_inc(p_hi, 1)

            def p_chunk(c, more):
                for i in range(NU):
                    p_square(c, i)
                for b in range(NL):
                    act.wait_ge(p_L, NL * c + (b + 1))
                    act.copy(lat[:, 0, b], ps[:, b, :]).then_inc(p_Lhi, 1)
                if more:
                    p_highs(c + 1, LOOP_BANKS)
                    p_rowcopy(c + 1)

            LOOP_BANKS, FIRST_BANKS = (2, 3, 0, 1), (4, 5, 4, 5)
            act.wait_ge(p_ef, NL)
            act.wait_ge(a_part3, 4 * NP2)
            act.wait_ge(a_vT, 2 * NP2)
            p_highs(0, FIRST_BANKS, (0, 1))
            a_exp_shifted(NP2 - 1, 1)
            act.wait_ge(p_rawu, 16)
            act.wait_ge(a_proj, 6 * NP2)
            for k in range(KB):
                if k == 2:
                    p_highs(0, FIRST_BANKS, (2, 3))
                act.copy(wup[:, 0, k], rawu[:, k]).then_inc(p_whi, 1)
            act.wait_ge(a_S, 2 * NP2)
            for l in range(NL):
                act.copy(wef[:, 0, l], ps[:, 7 - l, :]).then_inc(p_efhi, 1)
            act.wait_ge(p_raws, 64)
            act.copy(wf1[:, 0], raw1[:]).then_inc(p_whi, 1)
            act.wait_ge(p_rawd, 16)
            act.wait_ge(p_wlo, KB)
            for k in range(0, NU, 2):
                act.copy(wdn[:, 0, k:k + 2], rawd[:, k:k + 2]).then_inc(p_whi, 1)
            act.wait_ge(p_wlo, 1 + KB + NU // 2)
            p_rowcopy(0)
            act.wait_ge(a_ctx, 2 * NP2 + 2)
            with act.Fori(0, B - 1) as c:
                p_chunk(c, True)
            p_chunk(B - 1, False)

        @block.vector
        def _(dve):
            ch = Chain(dve, s_vch)
            M_LINKS, A_LINKS, P_LINKS = 51, 22, 89

            def rsqrt(n):
                v, m = mv[:, 0:n, 1], mv[:, 0:n, 0]
                r, h, t = rs[:, 0:n], hv[:, 0:n], nm[:, 0:n]
                ch.link(dve.tensor_scalar(h, v, EPS, None, ALU.add))
                ch.link(dve.tensor_scalar(t.bitcast(I32), h.bitcast(I32), 1, None, ALU.arith_shift_right))
                ch.link(dve.tensor_scalar(t.bitcast(I32), t.bitcast(I32), -1, None, ALU.bitwise_xor))
                dve.sem_inc(s_settled, 1)
                ch.link(dve.tensor_tensor(r.bitcast(I32), t.bitcast(I32), magic[:, 0:1].broadcast_to([P, n]), ALU.add))
                ch.link(dve.tensor_scalar(h, h, -0.5, None, ALU.mult))
                for _ in range(3):
                    ch.link(dve.tensor_tensor(t, r, r, ALU.mult))
                    ch.link(dve.tensor_tensor(t, t, h, ALU.mult))
                    ch.link(dve.scalar_tensor_tensor(out=r, in0=t, scalar=1.5, in1=r, op0=ALU.add, op1=ALU.mult))
                return dve.scalar_tensor_tensor(out=t, in0=m, scalar=-1.0, in1=r, op0=ALU.mult, op1=ALU.mult)

            ch.link(dve.memset(magic, RSQRT_MAGIC + 1))
            for lb in range(KB):
                dve.wait_ge(s_xt, B * lb + B)
                for n in range(B):
                    for m in range(n + 1, B):
                        ch.link(dve.tensor_tensor_reduce(dump[:, 0], xT[:, lb, n, :], xT[:, lb, m, :], 1.0, 0.0,
                                                         ALU.mult, ALU.add, sc[:, lb, n, m:m + 1]))
            for n in range(B):
                for m in range(n + 1, B):
                    ch.link(dve.tensor_copy(sc[:, :, m, n], sc[:, :, n, m]))
            dve.wait_ge(s_sq, B * KB)
            sc3 = small[:, 0:64].rearrange("p (r m) -> p r m", m=B)
            ch.link(dve.tensor_reduce(mx, sc3, X, ALU.max))
            dve.tensor_tensor(sc3, sc3, mx.unsqueeze(2).broadcast_to([P, KB * B, B]),
                              ALU.subtract).then_inc(s_pexp_in, 1)
            dve.wait_ge(s_pexp, 1)
            ch.link(dve.tensor_reduce(mx, sc3, X, ALU.add))
            ch.link(dve.reciprocal(mx, mx))
            ch.link(dve.tensor_tensor(sc3, sc3, mx.unsqueeze(2).broadcast_to([P, KB * B, B]), ALU.mult))
            for n in range(B):
                ins = dve.tensor_scalar(sc[:, :, n, n], sc[:, :, n, n], 2.0, None, ALU.add)
                if n < B - 1:
                    ch.link(ins)
                else:
                    ins.then_inc(s_mixw, 1)
            dve.wait_ge(s_mixw, 1)

            def mix(blocks):
                for n, lb in blocks:
                    dve.wait_ge(s_y0, KB * n + lb + 1)
                    for m in range(1, B):
                        ins = dve.scalar_tensor_tensor(out=yT[:, n, lb, :], in0=xT[:, lb, m, :],
                                                       scalar=sc[:, lb, n, m:m + 1], in1=yT[:, n, lb, :],
                                                       op0=ALU.mult, op1=ALU.add)
                        if m < B - 1:
                            ch.link(ins)
                        else:
                            ins.then_inc(s_y, 1)

            def norm1(n):
                dve.wait_ge(s_ycp, KB * (n + 1))
                for t in range(TB):
                    ins = dve.bn_stats(stats4[:, t], xs[:, TB * n + t])
                ch.link(ins)
                for t in range(TB):
                    ins = dve.bn_aggr(mv[:, t], stats4[:, t])
                ch.link(ins)
                ch.link(rsqrt(TB))
                for t in range(TB):
                    dve.tensor_scalar(xs[:, TB * n + t], xs[:, TB * n + t], rs[:, t:t + 1], nm[:, t:t + 1],
                                      ALU.mult, ALU.add).then_inc(s_x1, 1)

            mix(VECTOR_MIXES[:5])
            norm1(0)
            mix(VECTOR_MIXES[5:7])

            def m_lows(c):
                for k in range(KB):
                    dve.wait_ge(m_Thi, KB * c + (k + 1))
                    dve.tensor_tensor(xth[:, 1, k], ps[:, k, :], xth[:, 0, k].bitcast(F32),
                                      ALU.subtract).then_inc(m_Tlo, 1)
                dve.wait_ge(m_abs, c + 1)
                dve.tensor_tensor(statin, absum.unsqueeze(2).broadcast_to([P, TB, 2]), vmask,
                                  ALU.mult).then_inc(m_stat, 1)

            def m_ratio(c):
                dve.wait_ge(m_statps, c + 1)
                ch.link(dve.tensor_copy(ratio[:, 0:2], ps[:, 7, 0:2]))
                ch.link(dve.tensor_scalar(ratio[:, 1:2], ratio[:, 1:2], 1e-8, None, ALU.add))
                ch.link(dve.reciprocal(ratio[:, 1:2], ratio[:, 1:2]))
                ch.link(dve.tensor_tensor(ratio[:, 2:3], ratio[:, 0:1], ratio[:, 1:2], ALU.mult))
                dve.scalar_tensor_tensor(out=gbias[0:E], in0=gw_last[0:E], scalar=ratio[0:E, 2:3],
                                         in1=gb_col[0:E], op0=ALU.mult, op1=ALU.add).then_inc(m_gbias, 1)

            def m_probs(c):
                over = tA.unsqueeze(2).broadcast_to([P, TB, E])
                dve.wait_ge(m_lps, c + 1)
                ch.link(dve.tensor_copy(pr, ps[:, 7, 0:4 * TB].rearrange("p (t e) -> p t e", e=4)[:, :, 0:E]))
                ch.link(dve.tensor_reduce(tA, pr, X, ALU.max))
                dve.tensor_tensor(pr, pr, over, ALU.subtract).then_inc(m_shift, 1)
                dve.wait_ge(m_exp, c + 1)
                ch.link(dve.tensor_reduce(tA, pr, X, ALU.add))
                ch.link(dve.reciprocal(tA, tA))
                dve.tensor_tensor(pr, pr, over, ALU.mult).then_inc(m_prob, 1)

            def m_ranks(c):
                dve.wait_ge(m_t0, c + 1)
                ch.link(dve.tensor_copy(rank, ps[:, 7, 0:E]))
                dve.tensor_tensor(cmp3[:, 0:1], rank[:, 0:1], rank[:, 1:2], ALU.is_ge)
                dve.tensor_tensor(cmp3[:, 1:2], rank[:, 0:1], rank[:, 2:3], ALU.is_ge)
                ch.link(dve.tensor_tensor(cmp3[:, 2:3], rank[:, 1:2], rank[:, 2:3], ALU.is_ge))
                ch.link(dve.tensor_tensor(rank[:, 0:1], cmp3[:, 0:1], cmp3[:, 1:2], ALU.add))
                dve.tensor_scalar(rank[:, 0:1], rank[:, 0:1], -1.0, 2.0, ALU.mult, ALU.add)
                dve.scalar_tensor_tensor(out=rank[:, 1:2], in0=cmp3[:, 0:1], scalar=1.0, in1=cmp3[:, 2:3],
                                         op0=ALU.add, op1=ALU.subtract)
                ch.link(dve.tensor_tensor(rank[:, 2:3], cmp3[:, 1:2], cmp3[:, 2:3], ALU.add))
                ch.link(dve.tensor_scalar(last3, rank, 2.0, None, ALU.is_equal))
                dve.scalar_tensor_tensor(out=left_out, in0=last3[:, 2:3], scalar=2.0, in1=last3[:, 1:2],
                                         op0=ALU.mult, op1=ALU.add).then_inc(m_out, 1)

            def m_coefs(c):
                ch.link(dve.tensor_reduce(top[:, 0], pr, X, ALU.max))
                ch.link(dve.tensor_tensor(tA, pr[:, :, 0], pr[:, :, 1], ALU.min))
                ch.link(dve.tensor_tensor(tB, pr[:, :, 0], pr[:, :, 1], ALU.max))
                ch.link(dve.tensor_tensor(tB, tB, pr[:, :, 2], ALU.min))
                ch.link(dve.tensor_tensor(top[:, 1], tA, tB, ALU.max))
                ch.link(dve.scalar_tensor_tensor(out=tA, in0=top[:, 0], scalar=1e-8, in1=top[:, 1],
                                                 op0=ALU.add, op1=ALU.add))
                ch.link(dve.reciprocal(tA, tA))
                ch.link(dve.tensor_tensor(top, top, tA.unsqueeze(1).broadcast_to([P, 2, TB]), ALU.mult))
                ch.link(dve.tensor_tensor(second, rank[:, 1:2], rank[:, 0:1], ALU.subtract))
                ch.link(dve.scalar_tensor_tensor(out=first, in0=second, scalar=last3[:, 0:1], in1=rank[:, 0:1],
                                                 op0=ALU.mult, op1=ALU.add))
                ch.link(dve.tensor_scalar(second, first, -1.0, 1.0, ALU.mult, ALU.add))
                for slot, other in ((0, second), (1, first)):
                    ch.link(dve.tensor_scalar(tA, top[:, 0], other, None, ALU.mult))
                    ch.link(dve.scalar_tensor_tensor(out=coef[:, slot], in0=top[:, 1],
                                                     scalar=(first, second)[slot], in1=tA,
                                                     op0=ALU.mult, op1=ALU.add))

            def m_add(c, slot, t):
                j = slot * TB + t
                dve.wait_ge(m_O, SL * TB * c + (j + 1))
                row = xs[:, TB * c + t]
                dve.scalar_tensor_tensor(out=row, in0=ps[:, 4 + j % OB, :], scalar=coef[:, slot, t:t + 1],
                                         in1=row, op0=ALU.mult, op1=ALU.add).then_inc(m_Oacc, 1)

            def m_norm(c):
                for t in range(TB):
                    dve.wait_ge(m_Oacc, SL * TB * c + (TB + OB + t + 1))
                    dve.sem_inc(s_settled, 1)
                    ch.link(dve.bn_stats(stats4[:, t], xs[:, TB * c + t]))
                    dve.sem_inc(s_settled, 1)
                    ch.link(dve.bn_aggr(mv[:, t], stats4[:, t]))
                ch.link(rsqrt(TB))
                for t in range(TB):
                    dve.tensor_scalar(xs[:, TB * c + t], xs[:, TB * c + t], rs[:, t:t + 1], nm[:, t:t + 1],
                                      ALU.mult, ALU.add).then_inc(m_x2, 1)

            def m_chunk(c, more):
                m_coefs(c)
                m_add(c, 0, 0)
                m_add(c, 0, 1)
                if more:
                    m_lows(c + 1)
                m_add(c, 0, 2)
                m_add(c, 0, 3)
                if more:
                    m_ratio(c + 1)
                else:
                    a_weight_lows(0)
                dve.wait_ge(m_Oacc, SL * TB * c + (TB + OB))
                m_add(c, 1, 0)
                if not more:
                    a_weight_lows(1)
                m_add(c, 1, 1)
                if more:
                    m_probs(c + 1)
                m_add(c, 1, 2)
                if more:
                    m_ranks(c + 1)
                m_add(c, 1, 3)
                if not more:
                    a_weight_lows(2)
                    a_lows(0)
                    return
                m_norm(c)

            def a_lows(p):
                for h in range(2):
                    dve.wait_ge(a_Thi, 2 * p + (h + 1))
                    dve.tensor_tensor(xt3[:, 1, 2 * h:2 * h + 2], ps[:, 4 + h, :].rearrange("p (k t) -> p k t", k=2),
                                      xt3[:, 0, 2 * h:2 * h + 2].bitcast(F32), ALU.subtract).then_inc(a_Tlo, 1)

            def a_weight_lows(j):
                for k in range(KB):
                    dve.wait_ge(a_whi, KB * j + k + 1)
                    dve.tensor_tensor(wqkv[:, j, 1, k], ps[:, k, :], wqkv[:, j, 0, k].bitcast(F32),
                                      ALU.subtract).then_inc(a_wlo, 1)

            dve.wait_ge(m_gwp, 1)
            ch.link(dve.memset(tA, 0.0))
            dve.memset(tA, 0.0).then_inc(m_Oacc, OB)
            m_lows(0)
            mix(VECTOR_MIXES[7:8])
            m_ratio(0)
            mix(VECTOR_MIXES[8:])
            m_probs(0)
            m_ranks(0)
            dve.wait_ge(s_y_pool, len(POOL_MIXES))
            ch.link(dve.memset(is_low, 0.0))
            for lo in (0, 32):
                ch.link(dve.tensor_reduce(is_low[lo:lo + 2 * E], ident[lo:lo + 2 * E, lo + E:lo + 2 * E], X, ALU.add))
            ch.link(dve.tensor_scalar(sign, is_low, 2.0, -1.0, ALU.mult, ALU.add))
            ch.link(dve.tensor_copy(bias_high[:], bias_raw[:]))
            ch.link(dve.tensor_scalar(bias_neg[:], bias_high[:].bitcast(F32), sign, None, ALU.mult))
            for lo in (0, 32):
                rows = slice(lo, lo + 2 * E)
                for e in range(E):
                    ch.link(dve.tensor_tensor(pick[rows, e], ident[rows, lo + e:lo + e + 1].broadcast_to([2 * E, P]),
                                              ident[rows, lo + E + e:lo + E + e + 1].broadcast_to([2 * E, P]),
                                              ALU.add))
            dve.scalar_tensor_tensor(out=bias_rows[:], in0=bias_raw[:], scalar=is_low, in1=bias_neg[:],
                                     op0=ALU.mult, op1=ALU.subtract).then_inc(m_b2, 1)
            for n in range(1, B):
                norm1(n)
            ch.end()
            with dve.Fori(0, B - 1) as c:
                ch.begin(c, M_LINKS)
                m_chunk(c, True)
            ch.end(B - 1)
            m_chunk(B - 1, False)
            ch.end()

            def a_softmax_shift(p, u):
                rows = ps[:, 2 * u:2 * u + 2, :].rearrange("p b (i t) -> p (b i) t", t=H)
                ch.link(dve.tensor_reduce(mx3[:, u], rows, X, ALU.max))
                dve.tensor_tensor(sh[:, u], rows, mx3[:, u].unsqueeze(2).broadcast_to([P, 32, H]),
                                  ALU.subtract).then_inc(a_shift, 1)

            def by_pairs(t):
                return t.rearrange("p (i j d) -> p i j d", j=2, d=DH)

            def part(t, u, n):
                return t[:, u, n].rearrange("p i d j -> p i j d")

            def a_split(p, i, first=False):
                u, j = i // 2, i % 2
                dst = (q3, k3)[j]
                dve.wait_ge(a_part1, 4 * p + (i + 1))
                if i >= 2 or not first:
                    dve.wait_ge(a_part3, 4 * p + (i - 1))
                dve.tensor_tensor(by_pairs(rest[:, j]), by_pairs(ps[:, PROJ_BANK[3 * u + j], :]), part(dst, u, 0),
                                  ALU.subtract).then_inc(a_rest, 1)
                dve.wait_ge(a_rest, 4 * p + (i + 1))
                dve.tensor_copy(part(dst, u, 1), by_pairs(rest[:, j])).then_inc(a_part2, 1)

            def variant(t, u, upper, lower):
                words = t[:, u].rearrange("p n i d j -> p n i (d j)").bitcast(I32)
                words_of_part = H // 2 * DH
                return bass.AP(tensor=words.tensor, offset=words.offset + upper * words_of_part,
                               ap=[words.ap[0], [DH, H // 2], [(lower - upper) * words_of_part, 2], [1, DH]])

            def pairs_last(t):
                return t.bitcast(I32).rearrange("p t i -> p i t")

            def a_turn_q(p, u, first=False):
                dve.wait_ge(a_part3, 4 * p + (2 * u + 1))
                if not first:
                    dve.wait_ge(a_diag, 16 * p + (8 * u - 8))
                for v, (upper, lower) in enumerate(((0, 1), (0, 2))):
                    dve.transpose(pairs_last(qT[u][:, v]), variant(q3, u, upper, lower)).then_inc(a_qT, 1)

            def a_diagonal(p, u, blocks=tuple((1, g) for g in range(G)), first=False):
                dve.wait_ge(a_qT, 4 * p + (2 * u + 2))
                if not first:
                    dve.wait_ge(a_S, 2 * p + u)
                for v, g in blocks:
                    rows = slice(32 * g, 32 * g + 32)
                    dve.tensor_copy(qdiag[rows, v, :, rows], qT[u][rows, v]).then_inc(a_diag, 1)

            def a_turn_k(p, u, first=False):
                dve.wait_ge(a_part3, 4 * p + (2 * u + 2))
                if not first:
                    dve.wait_ge(a_S, 2 * p + (u - 1))
                for v, (upper, lower) in enumerate(((0, 0), (1, 1), (2, 0))):
                    dve.transpose(pairs_last(kT[:, u, v]), variant(k3, u, upper, lower)).then_inc(a_kT, 1)

            def a_turn_v(p, u):
                dve.wait_ge(a_v, 2 * p + (u + 1))
                dve.transpose(vT[:, u, 0:DH], vs[:, u].rearrange("p (t d) -> p d t", d=DH)).then_inc(a_vT, 1)

            def a_turn_probs(p, u):
                dve.wait_ge(a_exp, 2 * p + (u + 1))
                dve.transpose(pT[:, u], sh[:, u]).then_inc(a_PT, 1)

            def a_finish(p):
                dve.wait_ge(a_PV, p + 1)
                inv = [mx3[:, u].rearrange("p (b i) -> p b i", b=2) for u in range(2)]
                got = [ps[:, 2 * u:2 * u + 2, 0:16 * (DH + 1)].rearrange("p b (i d) -> p b i d", d=DH + 1)
                       for u in range(2)]
                dve.reciprocal(inv[0], got[0][:, :, :, DH])
                ch.link(dve.reciprocal(inv[1], got[1][:, :, :, DH]))
                for u in range(2):
                    dve.tensor_tensor(ctxs[:, u].rearrange("p (b i) d -> p b i d", b=2), got[u][:, :, :, 0:DH],
                                      inv[u].unsqueeze(3).broadcast_to([P, 2, 16, DH]), ALU.mult).then_inc(a_ctx, 1)
                for u in range(2):
                    dve.wait_ge(a_ctx, 2 * p + (u + 3))
                    ins = dve.transpose(attn[:, u].rearrange("p (h d) -> p d h", d=DH),
                                        ctxs[:, u].rearrange("p i d -> p d i"))
                ch.link(ins)

            def a_norm(p):
                for u in range(2):
                    ins = dve.tensor_tensor(attn[:, u], attn[:, u], xs[:, 2 * p + u], ALU.add)
                ch.link(ins)
                dve.bn_stats(stats4[:, 0], attn[:, 0])
                ch.link(dve.bn_stats(stats4[:, 1], attn[:, 1]))
                dve.sem_inc(s_settled, 1)
                dve.bn_aggr(mv[:, 0], stats4[:, 0])
                ch.link(dve.bn_aggr(mv[:, 1], stats4[:, 1]))
                ch.link(rsqrt(2))
                for u in range(2):
                    dve.tensor_scalar(xs[:, 2 * p + u], attn[:, u], rs[:, u:u + 1], nm[:, u:u + 1],
                                      ALU.mult, ALU.add).then_inc(a_x3, 1)

            def a_softmax(p, u):
                dve.wait_ge(a_S, 2 * p + (u + 1))
                a_softmax_shift(p, u)

            def a_pair(p, more_T, more_norm=True):
                a_diagonal(p, 1)
                a_softmax(p, 0)
                a_split(p + 1, 0)
                a_split(p + 1, 1)
                a_turn_q(p + 1, 0)
                a_turn_probs(p, 0)
                a_turn_k(p + 1, 0)
                a_diagonal(p + 1, 0)
                a_softmax(p, 1)
                a_split(p + 1, 2)
                a_turn_probs(p, 1)
                a_split(p + 1, 3)
                a_turn_q(p + 1, 1)
                a_turn_k(p + 1, 1)
                if more_T:
                    a_lows(p + 2)
                if more_norm:
                    a_norm(p - 1)
                a_finish(p)
                a_turn_v(p + 1, 0)
                a_turn_v(p + 1, 1)

            def p_lows(c, banks, blocks=range(KB)):
                for k in blocks:
                    dve.wait_ge(p_Thi, KB * c + (k + 1))
                    dve.tensor_tensor(xth[:, 1, k], ps[:, banks[k], :], xth[:, 0, k].bitcast(F32),
                                      ALU.subtract).then_inc(p_Tlo, 1)

            LOOP_BANKS, FIRST_BANKS = (2, 3, 0, 1), (4, 5, 4, 5)
            dve.memset(tB, 0.0).then_inc(a_ctx, 2)
            for u in range(2):
                a_split(0, 2 * u, first=True)
                a_split(0, 2 * u + 1, first=True)
                a_turn_q(0, u, first=True)
                if u == 0:
                    dve.wait_ge(a_const, 2)
                    a_diagonal(0, 0, first=True)
                a_turn_k(0, u, first=True)
            a_lows(1)
            a_turn_v(0, 0)
            a_turn_v(0, 1)
            m_norm(B - 1)
            ch.end()
            a_pair(0, True, more_norm=False)
            ch.end()
            with dve.Fori(0, NP2 - 3) as p:
                ch.begin(p, A_LINKS)
                a_pair(p + 1, True)
            ch.end(NP2 - 3)
            a_pair(NP2 - 2, False)
            a_diagonal(NP2 - 1, 1, ((0, 2), (0, 3), (1, 0), (1, 1), (1, 2), (1, 3)))
            a_softmax(NP2 - 1, 0)
            a_turn_probs(NP2 - 1, 0)
            p_lows(0, FIRST_BANKS, (0, 1))
            a_softmax(NP2 - 1, 1)
            a_turn_probs(NP2 - 1, 1)
            p_lows(0, FIRST_BANKS, (2, 3))
            for l in range(NL):
                dve.wait_ge(p_efhi, l + 1)
                dve.tensor_tensor(wef[:, 1, l], ps[:, 7 - l, :], wef[:, 0, l].bitcast(F32),
                                  ALU.subtract).then_inc(p_eflo, 1)
            a_norm(NP2 - 2)
            a_finish(NP2 - 1)
            a_norm(NP2 - 1)
            ch.end()

            def p_route(c):
                dve.wait_ge(p_lps, c + 1)
                dve.tensor_copy(logit8, ps[:, 7, 0:TB * NE].rearrange("p (t e) -> p t e", e=NE)).then_inc(p_top, 1)
                dve.wait_ge(p_top, c + 1)
                for t in range(TB):
                    dve.sem_inc(s_settled, 1)
                    ch.link(dve.max(top8[:, t], logit8[:, t]))
                ch.link(dve.tensor_tensor(route, top8[:, :, 0], top8[:, :, 1], ALU.add))

            def p_statistics(u, t):
                ch.link(dve.bn_stats(stats4[:, u], acc4[:, t]))
                dve.sem_inc(s_settled, 1)
                ch.link(dve.bn_aggr(mv[:, u], stats4[:, u]))

            def p_norms(c, tiles):
                ch.link(rsqrt(len(tiles)))
                for u, t in enumerate(tiles):
                    y = acc4[:, t]
                    ch.link(dve.scalar_tensor_tensor(out=y, in0=y, scalar=mv[:, u, 0:1], in1=gam_b[:],
                                                     op0=ALU.subtract, op1=ALU.mult))
                    dve.wait_ge(p_xb, TB * c + (t + 1))
                    ch.link(dve.scalar_tensor_tensor(out=y, in0=y, scalar=rs[:, u:u + 1], in1=xs[:, TB * c + t],
                                                     op0=ALU.mult, op1=ALU.add))
                for u, t in enumerate(tiles):
                    p_statistics(u, t)
                ch.link(rsqrt(len(tiles)))
                for u, t in enumerate(tiles):
                    dve.tensor_scalar(acc4[:, t], acc4[:, t], rs[:, u:u + 1], nm[:, u:u + 1],
                                      ALU.mult, ALU.add).then_inc(p_y, 1)

            def p_add_routed(c, t):
                dve.wait_ge(p_R, TB * c + (t + 1))
                dve.tensor_scalar(acc4[:, t], ps[:, 6, :], route[:, t:t + 1], None, ALU.mult).then_inc(p_Radd, 1)

            def p_chunk(c, more):
                p_route(c)
                for b in range(NL):
                    dve.wait_ge(p_Lhi, NL * c + (b + 1))
                    dve.tensor_tensor(lat[:, 1, b], ps[:, b, :], lat[:, 0, b].bitcast(F32),
                                      ALU.subtract).then_inc(p_Llo, 1)
                if more:
                    p_lows(c + 1, LOOP_BANKS)
                dve.wait_ge(s_out, 16 * TB * c + 1)
                p_add_routed(c, 0)
                for t in range(TB):
                    dve.wait_ge(p_Radd, TB * c + (t + 2))
                    dve.wait_ge(p_D, TB * c + (t + 1))
                    dve.tensor_tensor(acc4[:, t], acc4[:, t], ps[:, 4 + t % 2, :], ALU.add).then_inc(p_Dadd, 1)
                    if t + 1 < TB:
                        p_add_routed(c, t + 1)
                    dve.wait_ge(p_Dadd, TB * c + (t + 3))
                    p_statistics(t % 2 if more else 0, t)
                    if not more:
                        p_norms(c, (t,))
                    elif t % 2:
                        p_norms(c, (t - 1, t))

            dve.wait_ge(a_x3, NT)
            ch.link(dve.memset(tB, 0.0))
            dve.memset(tA, 0.0).then_inc(p_Dadd, 2)
            dve.memset(top, 0.0).then_inc(p_Radd, 1)
            ch.end()
            with dve.Fori(0, B - 1) as c:
                ch.begin(c, P_LINKS)
                p_chunk(c, True)
            ch.end(B - 1)
            p_chunk(B - 1, False)
            ch.end()


_INS = ['L0_attn_x', 'L0_ffn_gate_w', 'L0_ffn_gate_b', 'L0_ffn_w1', 'L0_ffn_b1', 'L0_ffn_w2', 'L0_ffn_b2',
        'L1_attn_wq', 'L1_attn_bq', 'L1_attn_wk', 'L1_attn_bk', 'L1_attn_wv', 'L1_attn_bv',
        'L1_ffn_gate_w', 'L1_ffn_up_w', 'L1_ffn_down_w', 'L1_ffn_fc1_w', 'L1_ffn_fc2_w', 'L1_ffn_expert_w',
        'L1_ffn_ln_gamma', 'L1_ffn_ln_beta']


def kernel(**inputs):
    import numpy as np
    import concourse.bacc as bacc
    from concourse.bass_utils import run_bass_kernel_spmd

    nc = bacc.Bacc("TRN2", target_bir_lowering=False, num_devices=1)
    arrays, args = {}, []
    for name in _INS:
        a = np.ascontiguousarray(inputs[name])
        arrays[f"in_{name}"] = a
        args.append(nc.dram_tensor(f"in_{name}", a.shape, mybir.dt.from_np(a.dtype), kind="ExternalInput").ap())
    out = nc.dram_tensor("out", (B, S, D), F32, kind="ExternalOutput").ap()
    build_program(nc, *args, out)
    r = run_bass_kernel_spmd(nc, [arrays], core_ids=[0])
    return r.results[0]["out"]
```
